# Optimizing a Trainium2 kernel written in Bass

```python
import numpy as np
import jax
import jax.numpy as jnp

def _softmax(x, axis=-1):
    return jax.nn.softmax(x, axis=axis)

def _gelu(x):
    return jax.nn.gelu(x, approximate=True)

def _silu(x):
    return jax.nn.silu(x)

def _sigmoid(x):
    return jax.nn.sigmoid(x)

def _layernorm(x, axis=-1, eps=1e-05):
    m = jnp.mean(x, axis=axis, keepdims=True)
    v = jnp.var(x, axis=axis, keepdims=True)
    return (x - m) / jnp.sqrt(v + eps)

def _scatter_add(tgt, idx, src, axis=0):
    return tgt.at[idx].add(src)

def _segment_sum(src, seg, n):
    return jax.ops.segment_sum(src, seg, n)
kernel_name = 'mk_adj_preln_d2_adj_r2_ecfc8c'

def setup_inputs(seed: int=0):
    np.random.seed(seed)
    _w = jnp.asarray

    def _rec_inputs():
        import jax
        import jax.numpy as jnp
        _gk = jax.random.key(seed)
        x = -0.0005146 + 1 * jax.random.normal(jax.random.fold_in(_gk, 1), (8, 1024, 128), jnp.float32)
        _a = jax.random.bernoulli(jax.random.fold_in(_gk, 2), 0.0078125, (8, 1024, 1024))
        adj = _a.astype(jnp.int32)
        return (x, adj)
    x, adj = _rec_inputs()

    def _L0_gnn_setup():
        import jax, jax.numpy as jnp
        import numpy as np
        B, N, C, OUT, S = (4, 1024, 128, 128, 25)
        DENSITY = 0.008
        key = jax.random.key(seed)
        kA, kX, kW = jax.random.split(key, 3)
        A = jax.random.bernoulli(kA, DENSITY, (B, N, N)).astype(jnp.int32)
        X = jax.random.normal(kX, (B, N, C), dtype=jnp.float32)
        W = jax.random.normal(kW, (2 * C, OUT), dtype=jnp.float32) * np.float32(1.0 / np.sqrt(2 * C))
        b = jnp.zeros((OUT,), dtype=jnp.float32)
        return {'A': A, 'X': X, 'W': W, 'b': b}
    _L0_gnn_all = _L0_gnn_setup()
    _L0_gnn_in = {k: v for k, v in _L0_gnn_all.items() if k in ('W', 'b')}
    del _L0_gnn_all

    def _L1_gnn_setup():
        import jax, jax.numpy as jnp
        import numpy as np
        DIM = 128
        HEADS = 8
        HEAD_DIM = DIM // HEADS
        DFF = 4 * DIM
        EPS = 1e-05

        def _layernorm(x, g, b):
            m = jnp.mean(x, axis=-1, keepdims=True)
            v = jnp.mean(jnp.square(x - m), axis=-1, keepdims=True)
            return (x - m) * jax.lax.rsqrt(v + EPS) * g + b
        key = jax.random.key(seed)
        ks = jax.random.split(key, 12)
        B, N = (8, 512)
        s = 1.0 / np.sqrt(DIM)
        x = jax.random.normal(ks[0], (B, N, DIM), dtype=jnp.float32)
        adj = jax.random.randint(ks[1], (B, N, N), 0, 2, dtype=jnp.int32)
        return {'x': x, 'adj': adj, 'Wqkv': jax.random.normal(ks[2], (3 * DIM, DIM), jnp.float32) * s, 'bqkv': jnp.zeros((3 * DIM,), jnp.float32), 'Wo': jax.random.normal(ks[3], (DIM, DIM), jnp.float32) * s, 'bo': jnp.zeros((DIM,), jnp.float32), 'ln1_g': jnp.ones((DIM,), jnp.float32), 'ln1_b': jnp.zeros((DIM,), jnp.float32), 'W1': jax.random.normal(ks[4], (DFF, DIM), jnp.float32) * s, 'b1': jnp.zeros((DFF,), jnp.float32), 'W2': jax.random.normal(ks[5], (DIM, DFF), jnp.float32) * (1.0 / np.sqrt(DFF)), 'b2': jnp.zeros((DIM,), jnp.float32), 'ln2_g': jnp.ones((DIM,), jnp.float32), 'ln2_b': jnp.zeros((DIM,), jnp.float32)}
    _L1_gnn_all = _L1_gnn_setup()
    _L1_gnn_in = {k: v for k, v in _L1_gnn_all.items() if k in ('Wqkv', 'bqkv', 'Wo', 'bo', 'ln1_g', 'ln1_b', 'W1', 'b1', 'W2', 'b2', 'ln2_g', 'ln2_b')}
    del _L1_gnn_all
    return {'x': x, 'adj': adj, 'L0_gnn_W': _L0_gnn_in['W'], 'L0_gnn_b': _L0_gnn_in['b'], 'L1_gnn_Wqkv': _L1_gnn_in['Wqkv'], 'L1_gnn_bqkv': _L1_gnn_in['bqkv'], 'L1_gnn_Wo': _L1_gnn_in['Wo'], 'L1_gnn_bo': _L1_gnn_in['bo'], 'L1_gnn_ln1_g': _L1_gnn_in['ln1_g'], 'L1_gnn_ln1_b': _L1_gnn_in['ln1_b'], 'L1_gnn_W1': _L1_gnn_in['W1'], 'L1_gnn_b1': _L1_gnn_in['b1'], 'L1_gnn_W2': _L1_gnn_in['W2'], 'L1_gnn_b2': _L1_gnn_in['b2'], 'L1_gnn_ln2_g': _L1_gnn_in['ln2_g'], 'L1_gnn_ln2_b': _L1_gnn_in['ln2_b']}

def reference(x, adj, L0_gnn_W, L0_gnn_b, L1_gnn_Wqkv, L1_gnn_bqkv, L1_gnn_Wo, L1_gnn_bo, L1_gnn_ln1_g, L1_gnn_ln1_b, L1_gnn_W1, L1_gnn_b1, L1_gnn_W2, L1_gnn_b2, L1_gnn_ln2_g, L1_gnn_ln2_b):
    import jax
    import jax.numpy as jnp

    def _L0_gnn_ref(A, X, W, b):
        import jax, jax.numpy as jnp
        import numpy as np
        B, N, C, OUT, S = (4, 1024, 128, 128, 25)
        DENSITY = 0.008
        mask = A != 0
        neg_inf = jnp.float32(-jnp.inf)
        pri = -jnp.arange(N, dtype=jnp.float32)
        scores = jnp.where(mask, pri, neg_inf)
        vals, idx = jax.lax.top_k(scores, S)
        valid = vals > neg_inf
        feats = jax.vmap(lambda x, i: x[i])(X, idx)
        feats = jnp.where(valid[..., None], feats, neg_inf)
        agg = feats.max(axis=2)
        degree = mask.sum(axis=-1)
        agg = jnp.where((degree <= S)[..., None], jnp.maximum(agg, 0.0), agg)
        h = jnp.concatenate([X, agg], axis=-1)
        out = jax.nn.relu(jnp.einsum('bnf,fo->bno', h, W) + b)
        return out

    def _L1_gnn_ref(x, adj, Wqkv, bqkv, Wo, bo, ln1_g, ln1_b, W1, b1, W2, b2, ln2_g, ln2_b):
        import jax, jax.numpy as jnp
        import numpy as np
        DIM = 128
        HEADS = 8
        HEAD_DIM = DIM // HEADS
        DFF = 4 * DIM
        EPS = 1e-05

        def _layernorm(x, g, b):
            m = jnp.mean(x, axis=-1, keepdims=True)
            v = jnp.mean(jnp.square(x - m), axis=-1, keepdims=True)
            return (x - m) * jax.lax.rsqrt(v + EPS) * g + b
        B, N, _ = x.shape
        eye = jnp.eye(N, dtype=bool)[None]
        allowed = (adj > 0) | (jnp.swapaxes(adj, 1, 2) > 0) | eye
        qkv = x @ Wqkv.T + bqkv
        q, k, v = jnp.split(qkv, 3, axis=-1)

        def heads(t):
            return t.reshape(B, N, HEADS, HEAD_DIM).transpose(0, 2, 1, 3)
        q, k, v = (heads(q), heads(k), heads(v))
        scale = 1.0 / np.sqrt(HEAD_DIM)
        scores = jnp.einsum('bhqd,bhkd->bhqk', q * scale, k)
        scores = jnp.where(allowed[:, None], scores, -jnp.inf)
        attn = jax.nn.softmax(scores, axis=-1)
        ctx = jnp.einsum('bhqk,bhkd->bhqd', attn, v)
        ctx = ctx.transpose(0, 2, 1, 3).reshape(B, N, DIM)
        attn_out = ctx @ Wo.T + bo
        x = _layernorm(x + attn_out, ln1_g, ln1_b)
        ff = jax.nn.relu(x @ W1.T + b1) @ W2.T + b2
        x = _layernorm(x + ff, ln2_g, ln2_b)
        return x
    h = jnp.maximum(_layernorm(x, axis=-1), 0.0)
    x = x + _L0_gnn_ref(adj, h, L0_gnn_W, L0_gnn_b)
    h = jnp.maximum(_layernorm(x, axis=-1), 0.0)
    x = x + _L1_gnn_ref(h, adj, L1_gnn_Wqkv, L1_gnn_bqkv, L1_gnn_Wo, L1_gnn_bo, L1_gnn_ln1_g, L1_gnn_ln1_b, L1_gnn_W1, L1_gnn_b1, L1_gnn_W2, L1_gnn_b2, L1_gnn_ln2_g, L1_gnn_ln2_b)
    return x

_drawn_inputs = setup_inputs


def setup_inputs(seed=0):
    import zlib

    import numpy as np

    out = dict(_drawn_inputs(seed))
    spreads = {'L0_gnn_b': (0.0, 0.1),
     'L1_gnn_bqkv': (0.0, 0.1),
     'L1_gnn_bo': (0.0, 0.1),
     'L1_gnn_ln1_g': (1.0, 0.2),
     'L1_gnn_ln1_b': (0.0, 0.1),
     'L1_gnn_b1': (0.0, 0.298),
     'L1_gnn_b2': (0.0, 0.1),
     'L1_gnn_ln2_g': (1.0, 0.2),
     'L1_gnn_ln2_b': (0.0, 0.1)}
    factors = {}
    for name, (base, spread) in spreads.items():
        noise = np.random.default_rng([zlib.crc32(name.encode()), seed]).standard_normal(out[name].shape)
        drawn = base * np.exp(spread * noise) if base else spread * noise
        out[name] = jnp.asarray(drawn.astype(out[name].dtype))
    for name, factor in factors.items():
        out[name] = (out[name] * factor).astype(out[name].dtype)
    return out
```

```python
import concourse.bass as bass
from concourse import mybir
from contextlib import ExitStack

fp32 = mybir.dt.float32
bf16 = mybir.dt.bfloat16
i32 = mybir.dt.int32
ALU = mybir.AluOpType
ACT = mybir.ActivationFunctionType
AX = mybir.AxisListType

B, N, C = 8, 1024, 128
P = 128
T = N // P
HALF = N // 2
TH = T // 2
S = 25
LW = 32
DEST, COUNT = 25, 26
HEADS, D = 8, 16
DFF = 4 * C
FC = DFF // P
EPS = 1e-5
SCALE = 1.0 / D ** 0.5
MASKED = -float(2 ** 100)
GROUP = 4
SPAN = P // GROUP
PAIRS = 2 * T
UNITS = 4
SAFE = (60.0 / SCALE) ** 2
SIZES = [4, 8, 12, 16, 20, 24, 25]
Q_PART = [0, 0, 1, 1, 0, 2]
K_PART = [0, 1, 0, 1, 2, 0]
SPLIT = len(Q_PART) * D
SHIFT = 3
MAGIC = float(0x5F3759DF)


class Chain:

    def __init__(self, eng, sem):
        self.eng, self.sem, self.n = eng, sem, 0

    def step(self, ins):
        ins.then_inc(self.sem, 1)
        self.n += 1

    def settle(self):
        self.eng.wait_ge(self.sem, self.n)

    def link(self, ins):
        self.step(ins)
        self.settle()


def program(nc, x, adj, L0_W, L0_b, Wqkv, bqkv, Wo, bo, ln1_g, ln1_b, W1, b1, W2, b2, ln2_g, ln2_b, out):
    h_table = [nc.dram_tensor(f"h_table_{i}", [N + 1, C], fp32).ap() for i in range(2)]
    lists = nc.dram_tensor("neighbour_lists", [N, LW], i32).ap()
    pooled = nc.dram_tensor("pooled_rows", [N, C], fp32).ap()
    parts_d = nc.dram_tensor("qk_parts", [3 * 2 * C, N], bf16).ap()

    ctx = ExitStack()
    with ctx:
        def sb(name, shape, dt=fp32):
            return ctx.enter_context(nc.sbuf_tensor(name, shape, dt))

        sem_ids = []

        def sem(name):
            s = ctx.enter_context(nc.semaphore(name))
            sem_ids.append(s.num)
            return s

        identf = sb("identf", [P, P])
        identb = sb("identb", [P, P], bf16)
        negident = sb("negident", [P, P], bf16)
        before = sb("before", [P, P], bf16)
        onesb = sb("onesb", [P, P], bf16)
        head_sum = sb("head_sum", [P, HEADS], bf16)
        prio_i = sb("prio_i", [P, N], i32)
        prio = prio_i[:, :].bitcast(fp32)
        node_i = sb("node_i", [P, T], i32)
        level_i = sb("level_i", [P, COUNT], i32)
        level = sb("level", [P, COUNT])
        w_l0 = sb("w_l0", [P, 2, C])
        wqkvT = sb("wqkvT", [P, 3 * C])
        woT = sb("woT", [P, C])
        w1T = sb("w1T", [P, DFF])
        w2T = sb("w2T", [P, FC, C])
        rows = sb("bias_rows", [P, 8, C])
        L0B, BV, BO, G1, B1R, B2, G2, B2R = range(8)
        bqk = sb("bqk", [P, 2])
        b1c = sb("b1c", [P, FC])

        xh = sb("xh", [P, T, C])
        adj_t = sb("adj_t", [P, 3, N], i32)
        vals = sb("vals", [P, T, LW])
        lst = sb("lst", [P, T, LW], i32)
        rank_i = sb("rank_i", [P, T], i32)
        onehot = sb("onehot", [P, T, COUNT], bf16)
        above = sb("above", [P, T, COUNT], bf16)
        abovesum = sb("abovesum", [P, COUNT], bf16)
        rprod = sb("rprod", [P, T, COUNT])
        cnt = sb("cnt", [P, T])
        flag4 = sb("flag4", [P, 2])
        flag4_i = sb("flag4_i", [1, 1], i32)
        st1 = sb("st1", [P, T, 6]); mv1 = sb("mv1", [P, T, 2]); nw1 = sb("nw1", [P, 5, T])
        st2 = sb("st2", [P, T, 6]); mv2 = sb("mv2", [P, T, 2]); nw2 = sb("nw2", [P, 5, T])
        lsorted = sb("lsorted", [P, T, LW], i32)
        nb = sb("nb", [P, 2, S, C])
        agg = sb("agg", [P, 2, C])
        xl = sb("xl", [P, T, C])
        x1 = sb("x1", [P, T, C])
        h2 = sb("h2", [P, T, C])
        qs = sb("qs", [P, HEADS, N], bf16)
        ks = sb("ks", [P, HEADS, N], bf16)
        va = sb("va", [P, T, HEADS, SPAN])
        m1 = sb("m1", [P, T, N], bf16)
        barred = sb("barred", [P, T, N], bf16)
        ctx_raw = sb("ctx_raw", [P, HALF])
        rden = sb("rden", [P, TH, GROUP])
        ctxn = sb("ctxn", [P, T, C])
        shift = sb("shift", [P, HEADS * T])
        shf = sb("shf", [HEADS * T, P])
        shr = sb("shr", [HEADS * T, P])
        shp = sb("shp", [HEADS * T, 3, P], bf16)
        nrm = sb("nrm", [HEADS, 4])
        nflag = sb("nflag", [1, 2])
        nflag_i = sb("nflag_i", [1, 1], i32)

        region = sb("region", [P, 12288])
        def view(at, shape):
            n = 1
            for k in shape:
                n *= k
            v = region[:, at:at + n]
            if len(shape) == 2:
                v = v.rearrange("p (a b) -> p a b", a=shape[0])
            return v
        hl = view(0, [T, C]); ag = view(1024, [T, C])
        resid = view(0, [2, N])
        hT = view(2048, [N]); aT = view(3072, [N])
        h2T = view(4096, [N])
        qkf = view(5120, [2, N])
        sq = region[:, 11264:12288].bitcast(bf16).rearrange("p (a n) -> p a n", a=2)
        sqb = region[:, 2048:3072].bitcast(bf16).rearrange("p (a n) -> p a n", a=2)
        parts = region[:, 7168:10240].bitcast(bf16).rearrange("p (j a n) -> p j a n", j=3, a=2)
        keys = view(0, [T, N])
        probs = region[:, 8192:12288].rearrange("p (j a n) -> p j a n", j=4, a=2)
        hid = view(0, [FC, N])
        ctxT = view(4096, [N])
        y = view(5120, [T, C])
        z = view(6144, [T, C])
        zT = view(7168, [N])
        y2 = view(8192, [T, C])
        wstage = region[:, 0:2048]

        sc = ctx.enter_context(nc.psum_tensor("sc", [P, 4, HALF], fp32))
        cb = ctx.enter_context(nc.psum_tensor("cb", [P, 2, HALF], fp32))
        ax = ctx.enter_context(nc.psum_tensor("ax", [P, 2, HALF], fp32))
        ax0, ax1 = ax[:, 0, :], ax[:, 1, :]

        s_w_in = sem("w_in")
        s_const_done = sem("const_done")
        s_wT_ready = sem("wT_ready")
        s_wT_used = sem("wT_used")
        s_setup_dve = sem("setup_dve")
        s_zero_out = sem("zero_out")
        s_dve_chain = sem("dve_chain")
        s_x_in = sem("x_in")
        s_rstd1 = sem("rstd1")
        s_h_ready = sem("h_ready")
        s_h_out = sem("h_out")
        s_adj_in0 = sem("adj_in0")
        s_adj_in1 = sem("adj_in1")
        s_adj_in2 = sem("adj_in2")
        s_adj_used = sem("adj_used")
        s_m1_ready = sem("m1_ready")
        s_need4 = sem("need4")
        s_need4_col = sem("need4_col")
        s_flag4_row = sem("flag4_row")
        s_rank_in = sem("rank_in")
        s_rank_counts = sem("rank_counts")
        s_ranks = sem("ranks")
        s_lists_out = sem("lists_out")
        s_lists_in = sem("lists_in")
        s_pool0 = sem("pool0")
        s_pool1 = sem("pool1")
        s_pool2 = sem("pool2")
        s_pool3 = sem("pool3")
        s_pool4 = sem("pool4")
        s_pool5 = sem("pool5")
        s_pool6 = sem("pool6")
        s_pool7 = sem("pool7")
        s_pooled_ready = sem("pooled_ready")
        s_pooled_out0 = sem("pooled_out0")
        s_pooled_out1 = sem("pooled_out1")
        s_nb_used = sem("nb_used")
        s_hl_in = sem("hl_in")
        s_ag_in = sem("ag_in")
        s_xl_in = sem("xl_in")
        s_hT_ready = sem("hT_ready")
        s_hT_sb = sem("hT_sb")
        s_aT_ready = sem("aT_ready")
        s_aT_sb = sem("aT_sb")
        s_lin_ready = sem("lin_ready")
        s_rstd2 = sem("rstd2")
        s_h2_ready = sem("h2_ready")
        s_h2T_ready = sem("h2T_ready")
        s_h2T_sb = sem("h2T_sb")
        s_q_ready = sem("q_ready")
        s_k_ready = sem("k_ready")
        s_v_ready = sem("v_ready")
        s_qk_f = sem("qk_f")
        s_part_ready = sem("part_ready")
        s_parts_out = sem("parts_out")
        s_qk_in = sem("qk_in")
        s_v_sb = sem("v_sb")
        s_sq_ready = sem("sq_ready")
        s_norms_ready = sem("norms_ready")
        s_norms_max = sem("norms_max")
        s_norm_row = sem("norm_row")
        s_nflag_ready = sem("nflag_ready")
        s_gscores = sem("gscores")
        s_gmax = sem("gmax")
        s_gshift = sem("gshift")
        s_gshift_row = sem("gshift_row")
        s_gshift_parts = sem("gshift_parts")
        s_shift_in = sem("shift_in")
        s_scores_ready = sem("scores_ready")
        s_probs_ready = sem("probs_ready")
        s_pv_done = sem("pv_done")
        s_ctx_sb = sem("ctx_sb")
        s_ctxT_raw = sem("ctxT_raw")
        s_ctxn_ready = sem("ctxn_ready")
        s_bar_counts = sem("bar_counts")
        s_bar_ready = sem("bar_ready")
        s_ctxT_ready = sem("ctxT_ready")
        s_ctxT_sb = sem("ctxT_sb")
        s_proj_ready = sem("proj_ready")
        s_rstd3 = sem("rstd3")
        s_z_norm = sem("z_norm")
        s_z_ready = sem("z_ready")
        s_zT_ready = sem("zT_ready")
        s_zT_sb = sem("zT_sb")
        s_hid_ready = sem("hid_ready")
        s_hid_sb = sem("hid_sb")
        s_ffn_ready = sem("ffn_ready")
        s_rstd4 = sem("rstd4")
        s_out_norm = sem("out_norm")
        s_out_ready = sem("out_ready")
        s_out_stored = sem("out_stored")
        sem_range = range(min(sem_ids), max(sem_ids) + 1)
        assert len(sem_range) == len(sem_ids)

        def clear_semaphores():
            nc.gpsimd.dma_reset()
            nc.gpsimd.sem_clear(sem_range)
            nc.all_engine_barrier()

        with nc.Block() as block:
            @block.sync
            def _(sp):
                sp.dma_start(w_l0[:, :, :], L0_W.rearrange("(a p) o -> p a o", p=P)).then_inc(s_w_in, 16)
                for j in range(3):
                    sp.dma_start(wstage[:, j * C:(j + 1) * C], Wqkv[j * C:(j + 1) * C, :]).then_inc(s_w_in, 16)
                sp.dma_start(wstage[:, 3 * C:4 * C], Wo[:, :]).then_inc(s_w_in, 16)
                for j in range(FC):
                    sp.dma_start(wstage[:, (4 + j) * C:(5 + j) * C], W1[j * C:(j + 1) * C, :]).then_inc(s_w_in, 16)
                sp.dma_start(wstage[:, 8 * C:12 * C], W2[:, :]).then_inc(s_w_in, 16)
                for j, v in ((L0B, L0_b), (BO, bo), (G1, ln1_g), (B1R, ln1_b), (B2, b2), (G2, ln2_g), (B2R, ln2_b)):
                    sp.dma_start(rows[:, j, :], v.rearrange("(a n) -> a n", a=1).to_broadcast([P, C])).then_inc(s_w_in, 16)
                sp.dma_start(rows[:, BV, :], bqkv[2 * C:3 * C].rearrange("(a n) -> a n", a=1).to_broadcast([P, C])).then_inc(s_w_in, 16)
                for j in range(2):
                    sp.dma_start(bqk[:, j:j + 1], bqkv[j * C:(j + 1) * C].rearrange("(p a) -> p a", a=1)).then_inc(s_w_in, 16)
                for j in range(FC):
                    sp.dma_start(b1c[:, j:j + 1], b1[j * C:(j + 1) * C].rearrange("(p a) -> p a", a=1)).then_inc(s_w_in, 16)
                sp.wait_ge(s_const_done, 1)
                for b in range(2):
                    sp.dma_start(h_table[b][N:N + 1, :], xh[0:1, 0, :]).then_inc(s_zero_out, 16)
                sp.wait_ge(s_zero_out, 32)
                sp.wait_ge(s_w_in, 16 * (1 + 3 + 1 + FC + 1 + 8 + 2 + FC))

            @block.gpsimd
            def _(pool):
                pool.memset(identf[:, :], 0.0)
                pool.memset(identb[:, :], 0.0)
                pool.memset(negident[:, :], 0.0)
                pool.memset(onesb[:, :], 1.0)
                pool.memset(before[:, :], 1.0)
                pool.memset(head_sum[:, :], 1.0).then_inc(s_setup_dve, 1)
                pool.wait_ge(s_setup_dve, 1)
                for m, v in ((identf, 1.0), (identb, 1.0), (negident, MASKED)):
                    pool.affine_select(out=m[:, :], in_=m[:, :], compare_op=ALU.not_equal, fill=v, base=0,
                                       pattern=[[-1, P]], channel_multiplier=1)
                pool.affine_select(out=before[:, :], in_=before[:, :], compare_op=ALU.is_gt, fill=0.0, base=0,
                                   pattern=[[1, P]], channel_multiplier=-1)
                pool.affine_select(out=head_sum[:, :], in_=head_sum[:, :], compare_op=ALU.is_ge, fill=0.0, base=0,
                                   pattern=[[-D, HEADS]], channel_multiplier=1).then_inc(s_setup_dve, 1)
                pool.wait_ge(s_setup_dve, 2)
                pool.affine_select(out=head_sum[:, :], in_=head_sum[:, :], compare_op=ALU.is_ge, fill=0.0, base=D - 1,
                                   pattern=[[D, HEADS]], channel_multiplier=-1)
                pool.iota(prio_i[:, :], pattern=[[-1, N]], base=N, channel_multiplier=0)
                pool.iota(node_i[:, :], pattern=[[P, T]], base=0, channel_multiplier=1)
                pool.iota(level_i[:, :], pattern=[[1, COUNT]], base=0, channel_multiplier=0).then_inc(s_setup_dve, 1)

            @block.vector
            def _(dve):
                nc.vector.memset(xh[:, 0, :], 0.0).then_inc(s_const_done, 1)
                nc.vector.memset(qs[96:128, :, :].rearrange("p h n -> p (h n)").bitcast(i32), 0)
                nc.vector.memset(ks[96:128, :, :], 1.0)
                nc.vector.memset(va[:, :, :, :], 1.0)
                nc.vector.memset(vals[:, :, :], 0.0)
                nc.vector.memset(lst[:, :, :], 0)
                nc.vector.memset(shift[:, :], 0.0)
                dve.wait_ge(s_setup_dve, 3)
                nc.vector.tensor_copy(prio, prio_i[:, :])
                nc.vector.tensor_copy(level[:, :], level_i[:, :])
                for g in range(3):
                    dve.wait_ge(s_wT_ready, g + 1)
                    if g == 0:
                        nc.vector.tensor_copy(wqkvT[:, :], sc[:, 0, 0:3 * C])
                        nc.vector.tensor_copy(woT[:, :], sc[:, 0, 3 * C:4 * C])
                    elif g == 1:
                        nc.vector.tensor_copy(w1T[:, :], sc[:, 1, :])
                    else:
                        nc.vector.tensor_copy(w2T[:, :, :], sc[:, 2, :].rearrange("p (c o) -> p c o", c=FC))

            @block.tensor
            def _(pe):
                pe.wait_ge(s_setup_dve, 2)
                pe.wait_ge(s_w_in, 16 * (1 + 3 + 1 + FC + 1 + 8 + 2 + FC))
                for g in range(3):
                    for j in range(4):
                        k = 4 * g + j
                        last = nc.tensor.transpose(sc[:, g, j * C:(j + 1) * C], wstage[:, k * C:(k + 1) * C], identf[:, :])
                    last.then_inc(s_wT_ready, 1)
        clear_semaphores()

        def rows_of(t):
            return t[0:N, :].rearrange("(t p) c -> p t c", p=P)

        def row_stats(ch, src, st, mv, w, done):
            for t in range(T):
                ch.step(nc.vector.bn_stats(st[:, t, :], src[:, t, :]))
            ch.settle()
            for t in range(T):
                ch.step(nc.vector.bn_aggr(mv[:, t, :], st[:, t, :]))
            ch.settle()
            v = mv[:, :, 1]
            ch.step(nc.vector.tensor_scalar(w[:, 0, :], v, EPS, None, ALU.add))
            ch.link(nc.vector.tensor_scalar(w[:, 1, :], v, EPS, 0.5, ALU.add, ALU.mult))
            ch.link(nc.vector.tensor_scalar(w[:, 3, :].bitcast(i32), w[:, 0, :].bitcast(i32), 1, None,
                                            ALU.logical_shift_right))
            ch.link(nc.vector.tensor_scalar(w[:, 2, :].bitcast(i32), w[:, 3, :].bitcast(i32), -1.0, MAGIC,
                                            ALU.mult, ALU.add))
            for _ in range(3):
                ch.link(nc.vector.tensor_tensor(w[:, 3, :], w[:, 2, :], w[:, 2, :], ALU.mult))
                ch.link(nc.vector.tensor_tensor(w[:, 3, :], w[:, 3, :], w[:, 1, :], ALU.mult))
                ch.link(nc.vector.scalar_tensor_tensor(out=w[:, 2, :], in0=w[:, 3, :], scalar=1.5, in1=w[:, 2, :],
                                                       op0=ALU.subtract, op1=ALU.mult))
            ch.step(nc.vector.tensor_scalar(w[:, 4, :], w[:, 2, :], -1.0, None, ALU.mult))
            nc.vector.tensor_tensor(w[:, 3, :], mv[:, :, 0], w[:, 2, :], ALU.mult).then_inc(done, 1)

        def slot(s, odd, first, pooling, main):
            block_ctx = nc.Block()
            block = block_ctx.__enter__()

            OUT = [s_pooled_out0, s_pooled_out1]
            ADJ = [s_adj_in0, s_adj_in1, s_adj_in2]
            order = []
            for t in range(T):
                if pooling:
                    order.append(("mask", t))
                if first:
                    order.append(("list", t))
            slot_of = {o: i for i, o in enumerate(order)}

            @block.sync
            def _(sp):
                if pooling:
                    sp.dma_start(lsorted[:, :, :], rows_of(lists)).then_inc(s_lists_in, 16)
                if main:
                    sp.dma_start(hl, rows_of(h_table[odd])).then_inc(s_hl_in, 16)
                    sp.dma_start(ag, rows_of(pooled)).then_inc(s_ag_in, 16)
                    sp.dma_start(xl[:, :, :], x[bass.ds(s, 1), :, :].rearrange("a (t p) c -> p (a t) c", p=P)).then_inc(s_xl_in, 16)
                if first:
                    sp.dma_start(xh[:, :, :], x[bass.ds(s + 2, 1), :, :].rearrange("a (t p) c -> p (a t) c", p=P)).then_inc(s_x_in, 16)

                def load_adj(i):
                    kind, t = order[i]
                    b = s + 2 if kind == "list" else s + 1
                    if i >= 3:
                        sp.wait_ge(s_adj_used, i - 2)
                    sp.dma_start(adj_t[:, i % 3, :], adj[bass.ds(b, 1), t * P:(t + 1) * P, :].rearrange("a p n -> p (a n)")).then_inc(ADJ[i % 3], 16)
                for i in range(min(3, len(order))):
                    load_adj(i)
                if main:
                    for j in range(3):
                        sp.wait_ge(s_part_ready, (4, 5, 6)[j])
                        sp.dma_start(parts_d[j * 2 * C:(j + 1) * 2 * C, :].rearrange("(a p) n -> p a n", p=P), parts[:, j, :, :]).then_inc(s_parts_out, 16)
                    sp.wait_ge(s_parts_out, 48)
                    for i in range(len(Q_PART)):
                        for a, dst, j in ((0, qs, Q_PART[i]), (1, ks, K_PART[i])):
                            r = (2 * j + a) * C
                            sp.dma_start(dst[i * D:(i + 1) * D, :, :], parts_d[r:r + C, :].rearrange("(h d) n -> d h n", d=D)).then_inc(s_qk_in, 16)
                    sp.wait_ge(s_nflag_ready, 1)
                    wide = sp.value_load(nflag_i[0:1, 0:1], min_val=0, max_val=1)
                    with sp.If(wide > 0):
                        sp.wait_ge(s_gshift_parts, 1)
                        for j in range(3):
                            sp.dma_start(qs[SPLIT + j:SPLIT + j + 1, :, :].rearrange("p h (t n) -> p (h t) n", t=T), shp[:, j, :]).then_inc(s_shift_in, 16)
                for i in range(3, len(order)):
                    load_adj(i)
                if first:
                    sp.wait_ge(s_h_ready, T)
                    if main:
                        sp.wait_ge(s_hl_in, 16)
                    sp.dma_start(rows_of(h_table[odd]), xh[:, :, :]).then_inc(s_h_out, 16)
                    sp.wait_ge(s_h_out, 16)
                if main:
                    sp.wait_ge(s_out_ready, 1)
                    sp.dma_start(out[bass.ds(s, 1), :, :].rearrange("a (t p) c -> p (a t) c", p=P), y2).then_inc(s_out_stored, 16)
                    sp.wait_ge(s_out_stored, 16)

            @block.gpsimd
            def _(pool):
                if pooling:
                    pool.wait_ge(s_lists_in, 16)
                    if main:
                        pool.wait_ge(s_ag_in, 16)
                    POOL = [s_pool0, s_pool1, s_pool2, s_pool3, s_pool4, s_pool5, s_pool6, s_pool7]

                    def send(t):
                        pool.wait_ge(s_pooled_ready, t + 1)
                        pool.indirect_dma_start(out=pooled[:, :], out_offset=bass.IndirectOffsetOnAxis(ap=lsorted[:, t, DEST:DEST + 1], axis=0),
                                                in_=agg[:, t % 2, :], in_offset=None).then_inc(OUT[t % 2], 16)
                    for t in range(T):
                        n = pool.value_load(lsorted[0:1, t, COUNT:COUNT + 1], min_val=0, max_val=S)
                        if t >= 2:
                            pool.wait_ge(s_nb_used, t - 1)

                        def gather(lo, hi):
                            for k in range(lo, hi):
                                pool.indirect_dma_start(out=nb[:, t % 2, k, :], out_offset=None, in_=h_table[1 - odd][:, :],
                                                        in_offset=bass.IndirectOffsetOnAxis(ap=lsorted[:, t, k:k + 1], axis=0)).then_inc(POOL[t], 16)
                        gather(0, SIZES[0])
                        for lo, hi in zip(SIZES, SIZES[1:]):
                            with pool.If(n > lo):
                                gather(lo, hi)
                        if t >= 1:
                            send(t - 1)
                    send(T - 1)
                    pool.wait_ge(s_pooled_out0, 16 * TH)
                    pool.wait_ge(s_pooled_out1, 16 * TH)
                if first:
                    pool.wait_ge(s_ranks, 2)
                    for t in range(T):
                        pool.indirect_dma_start(out=lists[:, :], out_offset=bass.IndirectOffsetOnAxis(ap=rank_i[:, t:t + 1], axis=0),
                                                in_=lst[:, t, :], in_offset=None).then_inc(s_lists_out, 16)
                    pool.wait_ge(s_lists_out, 16 * T)

            @block.vector
            def _(dve):
                ch = Chain(dve, s_dve_chain)
                POOL = [s_pool0, s_pool1, s_pool2, s_pool3, s_pool4, s_pool5, s_pool6, s_pool7]

                def before_attention():
                    dve.wait_ge(s_aT_ready, 2)
                    for h in range(2):
                        nc.vector.tensor_copy(aT[:, h * HALF:(h + 1) * HALF], sc[:, 2 + h, :]).then_inc(s_aT_sb, 1)
                    dve.wait_ge(s_xl_in, 16)
                    bias = rows[:, L0B:L0B + 1, :].to_broadcast([P, TH, C])
                    for h in range(2):
                        dve.wait_ge(s_lin_ready, h + 1)
                        ch.step(nc.vector.tensor_tensor(x1[:, h * TH:(h + 1) * TH, :], ax[:, h, :].rearrange("p (t c) -> p t c", t=TH), bias, ALU.add))
                    ch.settle()
                    ch.link(nc.vector.scalar_tensor_tensor(out=x1[:, :, :], in0=x1[:, :, :], scalar=0.0, in1=xl[:, :, :], op0=ALU.max, op1=ALU.add))
                    row_stats(ch, x1, st2, mv2, nw2, s_rstd2)
                    dve.wait_ge(s_qk_f, 4)
                    dve.wait_ge(s_part_ready, 4)
                    ch.link(nc.vector.tensor_tensor(resid, qkf, parts[:, 0, :, :], ALU.subtract))
                    nc.vector.tensor_copy(parts[:, 1, :, :], resid).then_inc(s_part_ready, 1)
                    dve.wait_ge(s_part_ready, 5)
                    nc.vector.tensor_tensor(parts[:, 2, :, :], resid, parts[:, 1, :, :], ALU.subtract).then_inc(s_part_ready, 1)
                    bv = rows[:, BV:BV + 1, :].rearrange("p a (h d) -> p a h d", d=D).to_broadcast([P, TH, HEADS, D])
                    for h in range(2):
                        dve.wait_ge(s_v_ready, h + 1)
                        nc.vector.tensor_tensor(va[:, h * TH:(h + 1) * TH, :, 0:D], cb[:, h, :].rearrange("p (t h d) -> p t h d", t=TH, d=D),
                                                bv, ALU.add).then_inc(s_v_sb, 1)
                    dve.wait_ge(s_norms_ready, 1)
                    ch.link(nc.vector.tensor_reduce(nrm[:, 0:2], sc[0:HEADS, :, :].rearrange("p (a b) n -> p a (b n)", a=2), AX.X, ALU.max))
                    nc.vector.tensor_tensor(nrm[:, 2:3], nrm[:, 0:1], nrm[:, 1:2], ALU.mult).then_inc(s_norms_max, 1)
                    dve.wait_ge(s_norm_row, 1)
                    ch.link(nc.vector.tensor_reduce(nflag[0:1, 0:1], ax0[0:1, 0:HEADS], AX.X, ALU.max))
                    nc.vector.tensor_scalar(nflag_i[0:1, 0:1], nflag[0:1, 0:1], SAFE, None, ALU.is_gt).then_inc(s_nflag_ready, 1)
                    dve.wait_ge(s_nflag_ready, 1)
                    wide = dve.value_load(nflag_i[0:1, 0:1], min_val=0, max_val=1)
                    with dve.If(wide > 0):
                        for i in range(HEADS * T):
                            dve.wait_ge(s_gscores, i + 1)
                            nc.vector.tensor_reduce(shift[:, i:i + 1], sc[:, 2 * (i % 2):2 * (i % 2) + 2, :].rearrange("p a n -> p (a n)"),
                                                    AX.X, ALU.max).then_inc(s_gmax, 1)
                        dve.wait_ge(s_gmax, HEADS * T)
                        nc.vector.tensor_scalar(shift[:, :], shift[:, :], -1.0, None, ALU.mult).then_inc(s_gshift, 1)
                        dve.wait_ge(s_gshift_row, 1)
                        nc.vector.tensor_copy(shf[:, :], ax0[0:HEADS * T, 0:P]).then_inc(s_gshift, 1)
                        dve.wait_ge(s_gshift, 2)
                        nc.vector.tensor_copy(shp[:, 0, :], shf[:, :]).then_inc(s_gshift, 1)
                        dve.wait_ge(s_gshift, 3)
                        nc.vector.tensor_tensor(shr[:, :], shf[:, :], shp[:, 0, :], ALU.subtract).then_inc(s_gshift, 1)
                        dve.wait_ge(s_gshift, 4)
                        nc.vector.tensor_copy(shp[:, 1, :], shr[:, :]).then_inc(s_gshift, 1)
                        dve.wait_ge(s_gshift, 5)
                        nc.vector.tensor_tensor(shp[:, 2, :], shr[:, :], shp[:, 1, :], ALU.subtract).then_inc(s_gshift_parts, 1)
                    return wide

                def adjacency(o):
                    i = slot_of[o]
                    dve.wait_ge(ADJ[i % 3], 16 * (i // 3 + 1))
                    return adj_t[:, i % 3, :]

                def mask_tile(t):
                    a = adjacency(("mask", t))
                    nc.vector.tensor_scalar(m1[:, t, :], a, 0.0, 1.0, ALU.max, ALU.min).then_inc(s_m1_ready, 1)
                    dve.wait_ge(s_m1_ready, t + 1)
                    dve.sem_inc(s_adj_used, 1)

                def list_tile(t):
                    a = adjacency(("list", t))
                    key = keys[:, t, :]
                    v = vals[:, t, :]
                    if t == 0 and main:
                        dve.wait_ge(s_parts_out, 48)
                    nc.vector.scalar_tensor_tensor(out=key, in0=a, scalar=0.0, in1=prio, op0=ALU.not_equal, op1=ALU.mult).then_inc(s_adj_used, 1)
                    dve.wait_ge(s_adj_used, slot_of[("list", t)] + 1)
                    for r in range(3):
                        ch.link(nc.vector.max(v[:, 8 * r:8 * r + 8], key))
                        ch.link(nc.vector.match_replace(out=key, in_to_replace=v[:, 8 * r:8 * r + 8], in_values=key, imm_value=0.0)) if r < 2 else None

                def pool_tile(t):
                    n = dve.value_load(lsorted[0:1, t, COUNT:COUNT + 1], min_val=0, max_val=S)
                    if t >= 2:
                        dve.wait_ge(OUT[t % 2], 16 * (t // 2))
                    for j, m in enumerate(SIZES):
                        low = SIZES[j - 1] if j else -1
                        with dve.If(n > low):
                            with dve.If(n < (m + 1)):
                                dve.wait_ge(POOL[t], 16 * m)
                                nc.vector.tensor_reduce(agg[:, t % 2, :], nb[:, t % 2, 0:m, :].rearrange("p k c -> p c k"), AX.X, ALU.max).then_inc(s_pooled_ready, 1)
                    dve.wait_ge(s_pooled_ready, t + 1)
                    dve.sem_inc(s_nb_used, 1)

                def fourth_round():
                    ch.link(nc.vector.tensor_reduce(flag4[:, 0:1], vals[:, :, 23:24].rearrange("p t a -> p (t a)"), AX.X, ALU.max))
                    nc.vector.tensor_copy(flag4[:, 1:2], flag4[:, 0:1]).then_inc(s_need4_col, 1)
                    ch.link(nc.vector.memset(vals[:, :, 24:32], 0.0))
                    dve.wait_ge(s_flag4_row, 1)
                    ch.link(nc.vector.tensor_reduce(flag4[0:1, 0:1], ax0[0:1, 0:P], AX.X, ALU.max))
                    ch.link(nc.vector.tensor_copy(flag4_i[0:1, 0:1], flag4[0:1, 0:1]))
                    more = dve.value_load(flag4_i[0:1, 0:1], min_val=0, max_val=N)
                    with dve.If(more > 0):
                        for t in range(T):
                            nc.vector.match_replace(out=keys[:, t, :], in_to_replace=vals[:, t, 16:24], in_values=keys[:, t, :], imm_value=0.0).then_inc(s_need4, 1)
                            dve.wait_ge(s_need4, 2 * t + 1)
                            nc.vector.max(vals[:, t, 24:32], keys[:, t, :]).then_inc(s_need4, 1)
                        dve.wait_ge(s_need4, 2 * T)

                def list_ranks():
                    ch.link(nc.vector.tensor_scalar(rprod[:, :, 0:S], vals[:, :, 0:S], 0.0, None, ALU.is_gt))
                    ch.link(nc.vector.tensor_reduce(cnt[:, :], rprod[:, :, 0:S], AX.X, ALU.add))
                    levels = level[:, :].rearrange("p (a v) -> p a v", a=1).to_broadcast([P, T, COUNT])
                    counts = cnt[:, :].rearrange("p (t a) -> p t a", a=1).to_broadcast([P, T, COUNT])
                    ch.link(nc.vector.tensor_tensor(above[:, :, :], counts, levels, ALU.is_gt))
                    ch.step(nc.vector.tensor_tensor(onehot[:, :, :], counts, levels, ALU.is_equal))
                    ch.link(nc.vector.tensor_reduce(rprod[:, 0, :], above[:, :, :].rearrange("p t v -> p v t"), AX.X, ALU.add))
                    nc.vector.tensor_copy(abovesum[:, :], rprod[:, 0, :]).then_inc(s_rank_in, 1)
                    ch.link(nc.vector.tensor_scalar(lst[:, :, 0:S], vals[:, :, 0:S], -1.0, float(N), ALU.mult, ALU.add))
                    ch.link(nc.vector.tensor_copy(lst[:, :, DEST:DEST + 1], node_i[:, :].rearrange("p (t a) -> p t a", a=1)))
                    nc.vector.tensor_copy(lst[:, :, COUNT:COUNT + 1], cnt[:, :].rearrange("p (t a) -> p t a", a=1)).then_inc(s_ranks, 1)
                    dve.wait_ge(s_rank_counts, 1)
                    dve.wait_ge(s_rank_in, 1)
                    ch.link(nc.vector.tensor_tensor(rprod[:, :, :], ax0[:, 0:T * COUNT].rearrange("p (t v) -> p t v", t=T), onehot[:, :, :], ALU.mult))
                    ch.link(nc.vector.tensor_reduce(cnt[:, :], rprod[:, :, :], AX.X, ALU.add))
                    nc.vector.tensor_copy(rank_i[:, :], cnt[:, :]).then_inc(s_ranks, 1)

                def context(u):
                    qh, g = divmod(u, 2)
                    dve.wait_ge(s_ctxT_raw, u + 1)
                    c = ax0.rearrange("p (t g d) -> p t g d", t=TH, g=GROUP)
                    ch.link(nc.vector.reciprocal(rden[:, :, :], c[:, :, :, D]))
                    r = rden[:, :, :].rearrange("p t (g a) -> p t g a", a=1).to_broadcast([P, TH, GROUP, D])
                    o = ctxn[:, qh * TH:(qh + 1) * TH, g * GROUP * D:(g + 1) * GROUP * D].rearrange("p t (g d) -> p t g d", d=D)
                    nc.vector.tensor_tensor(o, c[:, :, :, 0:D], r, ALU.mult).then_inc(s_ctxn_ready, 1)

                def row(j):
                    return rows[:, j:j + 1, :].to_broadcast([P, T, C])

                def after_attention():
                    for h in range(2):
                        dve.wait_ge(s_proj_ready, h + 1)
                        ch.step(nc.vector.tensor_tensor(y[:, h * TH:(h + 1) * TH, :], sc[:, 2 + h, :].rearrange("p (t c) -> p t c", t=TH),
                                                        rows[:, BO:BO + 1, :].to_broadcast([P, TH, C]), ALU.add))
                    ch.settle()
                    ch.link(nc.vector.tensor_tensor(y, y, h2[:, :, :], ALU.add))
                    row_stats(ch, y, st2, mv2, nw2, s_rstd3)
                    dve.wait_ge(s_z_norm, T)
                    ch.link(nc.vector.tensor_tensor(z, z, row(G1), ALU.mult))
                    nc.vector.tensor_tensor(z, z, row(B1R), ALU.add).then_inc(s_z_ready, 1)
                    if pooling:
                        pool_tile(6)
                        pool_tile(7)
                    dve.wait_ge(s_z_ready, 1)
                    for h in range(2):
                        dve.wait_ge(s_ffn_ready, h + 1)
                        ch.step(nc.vector.tensor_tensor(y[:, h * TH:(h + 1) * TH, :], cb[:, h, :].rearrange("p (t c) -> p t c", t=TH),
                                                        rows[:, B2:B2 + 1, :].to_broadcast([P, TH, C]), ALU.add))
                    ch.settle()
                    ch.link(nc.vector.tensor_tensor(y, y, z, ALU.add))
                    row_stats(ch, y, st2, mv2, nw2, s_rstd4)
                    dve.wait_ge(s_out_norm, T)
                    ch.link(nc.vector.tensor_tensor(y2, y2, row(G2), ALU.mult))
                    ch.link(nc.vector.tensor_tensor(y2, y2, row(B2R), ALU.add))
                    nc.vector.tensor_tensor(y2, y2, x1[:, :, :], ALU.add).then_inc(s_out_ready, 1)

                if main:
                    wide = before_attention()
                if first:
                    dve.wait_ge(s_x_in, 16)
                    row_stats(ch, xh, st1, mv1, nw1, s_rstd1)
                for t in range(T):
                    if pooling:
                        mask_tile(t)
                    if first:
                        list_tile(t)
                    if pooling and t >= 2 and t != 4:
                        pool_tile(t - 2 - (t > 4))
                    if main and t in (3, 6):
                        context(0 if t == 3 else 1)
                if main:
                    context(2)
                if first:
                    fourth_round()
                    list_ranks()
                if pooling:
                    for t in range(5, T if not main else 6):
                        pool_tile(t)
                if main:
                    context(3)
                    after_attention()
                    with dve.If(wide > 0):
                        dve.wait_ge(s_out_ready, 1)
                        nc.vector.memset(qs[96:128, :, :].rearrange("p h n -> p (h n)").bitcast(i32), 0)

            @block.scalar
            def _(act):
                def norm(dst, src, func, w, t, done):
                    nc.scalar.activation(dst[:, t, :], src[:, t, :], func, bias=w[:, 3, t:t + 1], scale=w[:, 4, t:t + 1]).then_inc(done, 1)

                def bar_tile(i):
                    half, kt = divmod(i, T)
                    act.wait_ge(s_bar_counts, i + 1)
                    nc.scalar.activation(barred[:, kt, half * HALF:(half + 1) * HALF], ax1, ACT.Relu, bias=1.0, scale=-1.0).then_inc(s_bar_ready, 1)

                def first_norm():
                    act.wait_ge(s_rstd1, 1)
                    for t in range(T):
                        norm(xh, xh, ACT.Relu, nw1, t, s_h_ready)

                if main:
                    for h in range(2):
                        act.wait_ge(s_hT_ready, h + 1)
                        nc.scalar.activation(hT[:, h * HALF:(h + 1) * HALF], sc[:, h, :], ACT.Copy).then_inc(s_hT_sb, 1)
                    act.wait_ge(s_rstd2, 1)
                    for t in range(T):
                        norm(h2, x1, ACT.Relu, nw2, t, s_h2_ready)
                    for h in range(2):
                        act.wait_ge(s_h2T_ready, h + 1)
                        nc.scalar.activation(h2T[:, h * HALF:(h + 1) * HALF], sc[:, h, :], ACT.Copy).then_inc(s_h2T_sb, 1)
                    for a, ready in ((0, s_q_ready), (1, s_k_ready)):
                        for h in range(2):
                            act.wait_ge(ready, h + 1)
                            src = ax[:, h, :] if a else sc[:, 2 + h, :]
                            cols = slice(h * HALF, (h + 1) * HALF)
                            nc.scalar.activation(qkf[:, a, cols], src, ACT.Identity, bias=bqk[:, a:a + 1]).then_inc(s_qk_f, 1)
                            nc.scalar.activation(parts[:, 0, a, cols], src, ACT.Identity, bias=bqk[:, a:a + 1]).then_inc(s_part_ready, 1)
                    act.wait_ge(s_qk_f, 4)
                    nc.scalar.activation(sq, qkf, ACT.Square).then_inc(s_sq_ready, 1)
                    if first:
                        first_norm()
                    for u in range(UNITS):
                        for j in range(PAIRS):
                            i = u * PAIRS + j
                            act.wait_ge(s_scores_ready, i + 1)
                            if i >= 4:
                                act.wait_ge(s_pv_done, (i - 4) // 2 + 1)
                            nc.scalar.activation(probs[:, i % 4, :, :], sc[:, 2 * (i % 2):2 * (i % 2) + 2, :], ACT.Exp, scale=SCALE).then_inc(s_probs_ready, 1)
                            if u >= 1 and j == 3:
                                if u >= 2:
                                    act.wait_ge(s_ctxT_raw, u - 1)
                                act.wait_ge(s_pv_done, u * T)
                                nc.scalar.activation(ctx_raw[:, :], cb[:, (u - 1) % 2, :], ACT.Copy).then_inc(s_ctx_sb, 1)
                            if pooling and u >= 2 and j % 4 == 2:
                                bar_tile((u - 2) * 4 + j // 4)
                    act.wait_ge(s_ctxT_raw, 3)
                    act.wait_ge(s_pv_done, UNITS * T)
                    nc.scalar.activation(ctx_raw[:, :], cb[:, 1, :], ACT.Copy).then_inc(s_ctx_sb, 1)
                    late = iter(range(T, 2 * T)) if pooling else iter(())

                    def bar_next(n):
                        for _ in range(n):
                            i = next(late, None)
                            if i is not None:
                                bar_tile(i)
                    bar_next(2)
                    for h in range(2):
                        act.wait_ge(s_ctxT_ready, h + 1)
                        nc.scalar.activation(ctxT[:, h * HALF:(h + 1) * HALF], sc[:, h, :], ACT.Copy).then_inc(s_ctxT_sb, 1)
                    bar_next(4)
                    act.wait_ge(s_rstd3, 1)
                    for t in range(T):
                        norm(z, y, ACT.Identity, nw2, t, s_z_norm)
                    for h in range(2):
                        act.wait_ge(s_zT_ready, h + 1)
                        nc.scalar.activation(zT[:, h * HALF:(h + 1) * HALF], sc[:, h, :], ACT.Copy).then_inc(s_zT_sb, 1)
                    for i in range(2 * FC):
                        h, c = divmod(i, FC)
                        act.wait_ge(s_hid_ready, i + 1)
                        nc.scalar.activation(hid[:, c, h * HALF:(h + 1) * HALF], sc[:, i % 4, :], ACT.Relu, bias=b1c[:, c:c + 1]).then_inc(s_hid_sb, 1)
                    bar_next(2)
                    act.wait_ge(s_rstd4, 1)
                    for t in range(T):
                        norm(y2, y, ACT.Identity, nw2, t, s_out_norm)
                else:
                    if first:
                        first_norm()
                    if pooling:
                        for i in range(2 * T):
                            bar_tile(i)

            @block.tensor
            def _(pe):
                def transposes(dst, src, h, done):
                    for t in range(TH):
                        last = nc.tensor.transpose(dst[:, t * C:(t + 1) * C], src[:, h * TH + t, :], identf[:, :])
                    last.then_inc(done, 1)

                def bar_counts(i):
                    half, kt = divmod(i, T)
                    pe.wait_ge(s_m1_ready, max(kt + 1, (half + 1) * TH))
                    if i:
                        pe.wait_ge(s_bar_ready, i)
                    nc.tensor.matmul(ax1, identb[:, :], m1[:, kt, half * HALF:(half + 1) * HALF], start=True, stop=False)
                    if kt // TH == half:
                        a = kt % TH * P
                        nc.tensor.matmul(ax1[:, a:a + P], identb[:, :], identb[:, :], start=False, stop=False)
                    for j in range(TH):
                        last = nc.tensor.matmul(ax1[:, j * P:(j + 1) * P], m1[:, half * TH + j, kt * P:(kt + 1) * P], identb[:, :],
                                                start=False, stop=(j == TH - 1))
                    last.then_inc(s_bar_counts, 1)

                def flag4_row():
                    pe.wait_ge(s_need4_col, 1)
                    if main:
                        pe.wait_ge(s_ctxn_ready, 3)
                    nc.tensor.transpose(ax0[0:1, 0:P], flag4[:, 1:2], identf[:, :]).then_inc(s_flag4_row, 1)

                def rank_counts():
                    pe.wait_ge(s_rank_in, 1)
                    for t in range(T):
                        o = ax0[:, t * COUNT:(t + 1) * COUNT]
                        nc.tensor.matmul(o, onesb[:, :], abovesum[:, :], start=True, stop=False)
                        for e in range(t):
                            nc.tensor.matmul(o, onesb[:, :], onehot[:, e, :], start=False, stop=False)
                        last = nc.tensor.matmul(o, before[:, :], onehot[:, t, :], start=False, stop=True)
                    last.then_inc(s_rank_counts, 1)

                def scores(i):
                    u, j = divmod(i, PAIRS)
                    qh, g = divmod(u, 2)
                    kt, pair = divmod(j, 2)
                    if i >= 2:
                        pe.wait_ge(s_probs_ready, i - 1)
                    q = slice(qh * HALF, (qh + 1) * HALF)
                    for a in range(2):
                        h = g * GROUP + pair * 2 + a
                        o = sc[:, 2 * (i % 2) + a, :]
                        nc.tensor.matmul(o, ks[0:SPLIT + SHIFT, h, kt * P:(kt + 1) * P], qs[0:SPLIT + SHIFT, h, q], start=True, stop=False)
                    for a in range(2):
                        o = sc[:, 2 * (i % 2) + a, :]
                        last = nc.tensor.matmul(o, negident[:, :], barred[:, kt, q], start=False, stop=True)
                    last.then_inc(s_scores_ready, 1)

                def contexts(i):
                    u, kt = divmod(i, T)
                    g = u % 2
                    if kt == 0 and u >= 2:
                        pe.wait_ge(s_ctx_sb, u - 1)
                    pe.wait_ge(s_probs_ready, 2 * i + 2)
                    for a in range(GROUP):
                        last = nc.tensor.matmul(cb[SPAN * a:SPAN * (a + 1), u % 2, :], va[:, kt, g * GROUP + a, :],
                                                probs[:, (2 * i + a // 2) % 4, a % 2, :], start=(kt == 0), stop=(kt == T - 1))
                    last.then_inc(s_pv_done, 1)

                def context_rows(u):
                    pe.wait_ge(s_ctx_sb, u + 1)
                    if u:
                        pe.wait_ge(s_ctxn_ready, u)
                    if u == 3 and first:
                        pe.wait_ge(s_ranks, 2)
                    for t in range(TH):
                        last = nc.tensor.transpose(ax0[:, t * P:(t + 1) * P], ctx_raw[:, t * P:(t + 1) * P], identf[:, :])
                    last.then_inc(s_ctxT_raw, 1)

                if main:
                    pe.wait_ge(s_hl_in, 16)
                    for h in range(2):
                        transposes(sc[:, h, :], hl, h, s_hT_ready)
                    pe.wait_ge(s_ag_in, 16)
                    for h in range(2):
                        transposes(sc[:, 2 + h, :], ag, h, s_aT_ready)
                    pe.wait_ge(s_hT_sb, 2)
                    pe.wait_ge(s_aT_sb, 2)
                    for h in range(2):
                        for t in range(TH):
                            cols = slice((h * TH + t) * P, (h * TH + t + 1) * P)
                            o = ax[:, h, t * C:(t + 1) * C]
                            nc.tensor.matmul(o, hT[:, cols], w_l0[:, 0, :], start=True, stop=False)
                            last = nc.tensor.matmul(o, aT[:, cols], w_l0[:, 1, :], start=False, stop=True)
                        last.then_inc(s_lin_ready, 1)
                    for h in range(2):
                        pe.wait_ge(s_h2_ready, (h + 1) * TH)
                        transposes(sc[:, h, :], h2, h, s_h2T_ready)
                    pe.wait_ge(s_h2T_sb, 2)
                    for h in range(2):
                        nc.tensor.matmul(sc[:, 2 + h, :], wqkvT[:, 0:C], h2T[:, h * HALF:(h + 1) * HALF], start=True, stop=True).then_inc(s_q_ready, 1)
                    for h in range(2):
                        nc.tensor.matmul(ax[:, h, :], wqkvT[:, C:2 * C], h2T[:, h * HALF:(h + 1) * HALF], start=True, stop=True).then_inc(s_k_ready, 1)
                    for h in range(2):
                        for t in range(TH):
                            cols = slice((h * TH + t) * P, (h * TH + t + 1) * P)
                            last = nc.tensor.matmul(cb[:, h, t * C:(t + 1) * C], h2T[:, cols], wqkvT[:, 2 * C:3 * C], start=True, stop=True)
                        last.then_inc(s_v_ready, 1)
                    pe.wait_ge(s_sq_ready, 1)
                    for a in range(2):
                        for h in range(2):
                            last = nc.tensor.matmul(sc[0:HEADS, 2 * a + h, :], head_sum[:, :], sq[:, a, h * HALF:(h + 1) * HALF], start=True, stop=True)
                    last.then_inc(s_norms_ready, 1)
                    pe.wait_ge(s_norms_max, 1)
                    nc.tensor.transpose(ax0[0:1, 0:HEADS], nrm[:, 2:3], identf[0:HEADS, 0:HEADS]).then_inc(s_norm_row, 1)
                    pe.wait_ge(s_qk_in, 2 * len(Q_PART) * 16)
                    pe.wait_ge(s_v_sb, 2)
                    pe.wait_ge(s_nflag_ready, 1)
                    wide = pe.value_load(nflag_i[0:1, 0:1], min_val=0, max_val=1)
                    with pe.If(wide > 0):
                        for i in range(HEADS * T):
                            h, qt = divmod(i, T)
                            if i >= 2:
                                pe.wait_ge(s_gmax, i - 1)
                            for a in range(2):
                                nc.tensor.matmul(sc[:, 2 * (i % 2) + a, :], qs[0:SPLIT, h, qt * P:(qt + 1) * P], ks[0:SPLIT, h, a * HALF:(a + 1) * HALF],
                                                 start=True, stop=False)
                                last = nc.tensor.matmul(sc[:, 2 * (i % 2) + a, :], negident[:, :], barred[:, qt, a * HALF:(a + 1) * HALF], start=False, stop=True)
                            last.then_inc(s_gscores, 1)
                        pe.wait_ge(s_gshift, 1)
                        nc.tensor.transpose(ax0[0:HEADS * T, 0:P], shift[:, :], identf[:, :]).then_inc(s_gshift_row, 1)
                        pe.wait_ge(s_shift_in, 48)

                    for i in range(UNITS * PAIRS):
                        u, j = divmod(i, PAIRS)
                        scores(i)
                        if i >= 2 and i % 2 == 0:
                            contexts(i // 2 - 1)
                        if u >= 1 and j == 5:
                            context_rows(u - 1)
                        if pooling and u >= 2 and j % 4 == 1:
                            bar_counts((u - 2) * 4 + j // 4)
                        if first and u == 3 and j == 10:
                            flag4_row()
                    contexts(UNITS * T - 1)
                    if first:
                        rank_counts()
                    if pooling:
                        bar_counts(T)
                    context_rows(3)
                    late = iter(range(T + 1, 2 * T)) if pooling else iter(())

                    def bar_next(n):
                        for _ in range(n):
                            i = next(late, None)
                            if i is not None:
                                bar_counts(i)
                    bar_next(1)
                    pe.wait_ge(s_ctxn_ready, 4)
                    for h in range(2):
                        transposes(sc[:, h, :], ctxn, h, s_ctxT_ready)
                    pe.wait_ge(s_ctxT_sb, 2)
                    for h in range(2):
                        for t in range(TH):
                            cols = slice((h * TH + t) * P, (h * TH + t + 1) * P)
                            last = nc.tensor.matmul(sc[:, 2 + h, t * C:(t + 1) * C], ctxT[:, cols], woT[:, :], start=True, stop=True)
                        last.then_inc(s_proj_ready, 1)
                    bar_next(4)
                    pe.wait_ge(s_z_ready, 1)
                    for h in range(2):
                        transposes(sc[:, h, :], z, h, s_zT_ready)
                    for i in range(2 * FC):
                        h, c = divmod(i, FC)
                        pe.wait_ge(s_zT_sb, h + 1)
                        if c == 0:
                            pe.wait_ge(s_zT_sb, 2)
                        if i >= 4:
                            pe.wait_ge(s_hid_sb, i - 3)
                        nc.tensor.matmul(sc[:, i % 4, :], w1T[:, c * P:(c + 1) * P], zT[:, h * HALF:(h + 1) * HALF], start=True, stop=True).then_inc(s_hid_ready, 1)
                    for h in range(2):
                        pe.wait_ge(s_hid_sb, (h + 1) * FC)
                        for t in range(TH):
                            cols = slice((h * TH + t) * P, (h * TH + t + 1) * P)
                            for c in range(FC):
                                last = nc.tensor.matmul(cb[:, h, t * C:(t + 1) * C], hid[:, c, cols], w2T[:, c, :], start=(c == 0), stop=(c == FC - 1))
                        last.then_inc(s_ffn_ready, 1)
                    bar_next(2)
                else:
                    if pooling:
                        for i in range(2 * T):
                            bar_counts(i)
                    if first:
                        flag4_row()
                        rank_counts()
            block_ctx.__exit__(None, None, None)
            clear_semaphores()

        slot(-2, 0, True, False, False)
        slot(-1, 1, True, True, False)
        with nc.Fori(0, (B - 2) // 2) as i:
            slot(i * 2, 0, True, True, True)
            slot(i * 2 + 1, 1, True, True, True)
        slot(B - 2, 0, False, True, True)
        slot(B - 1, 1, False, False, True)


_INS = ['x', 'adj', 'L0_gnn_W', 'L0_gnn_b', 'L1_gnn_Wqkv', 'L1_gnn_bqkv', 'L1_gnn_Wo', 'L1_gnn_bo', 'L1_gnn_ln1_g', 'L1_gnn_ln1_b',
        'L1_gnn_W1', 'L1_gnn_b1', 'L1_gnn_W2', 'L1_gnn_b2', 'L1_gnn_ln2_g', 'L1_gnn_ln2_b']
_OUTS = [((B, N, C), 'float32')]


def kernel(**inputs):
    import numpy as _np
    import concourse.bacc as _bacc
    from concourse import mybir as _mybir
    from concourse.bass_utils import run_bass_kernel_spmd as _run

    nc = _bacc.Bacc("TRN2", target_bir_lowering=False, num_devices=1)
    arrays, args = {}, []
    for name in _INS:
        a = _np.ascontiguousarray(inputs[name])
        arrays[f"in_{name}_dram"] = a
        args.append(nc.dram_tensor(f"in_{name}_dram", a.shape, _mybir.dt.from_np(a.dtype), kind="ExternalInput").ap())
    for i, (shape, dtype) in enumerate(_OUTS):
        dt = _mybir.dt.from_np(_np.dtype(dtype))
        args.append(nc.dram_tensor(f"out_{i}_dram", shape, dt, kind="ExternalOutput").ap())
    program(nc, *args)
    r = _run(nc, [arrays], core_ids=[0])
    return r.results[0]["out_0_dram"]
```

```python
import concourse.bass as bass
from concourse import mybir
from contextlib import ExitStack

fp32 = mybir.dt.float32
bf16 = mybir.dt.bfloat16
i32 = mybir.dt.int32
ALU = mybir.AluOpType
ACT = mybir.ActivationFunctionType
AX = mybir.AxisListType

B, N, C = 8, 1024, 128
P = 128
T = N // P
HALF = N // 2
TH = T // 2
S = 25
LW = 32
DEST, COUNT = 25, 26
HEADS, D = 8, 16
DFF = 4 * C
FC = DFF // P
EPS = 1e-5
SCALE = 1.0 / D ** 0.5
MASKED = -float(2 ** 100)
GROUP = 4
SPAN = P // GROUP
PAIRS = 2 * T
UNITS = 4
SAFE = (60.0 / SCALE) ** 2
CHUNKS = 8
CW = N // CHUNKS
SIZES = [4, 8, 12, 16, 20, 24, 25]
Q_PART = [0, 0, 1, 1, 0, 2]
K_PART = [0, 1, 0, 1, 2, 0]
SPLIT = len(Q_PART) * D
SHIFT = 3
MAGIC = float(0x5F3759DF)
POOL_AFTER = {1: 4, 2: 5, 4: 6, 5: 7}
CONTEXT_AFTER = {3: 0, 6: 1}
ROWS_AT = {1: 5, 2: 5, 3: 11}
FIRST_NORM_AT = 24
FULL_AT = 50
RANKS_AT = 54


class Chain:

    def __init__(self, eng, sem):
        self.eng, self.sem, self.n = eng, sem, 0

    def step(self, ins):
        ins.then_inc(self.sem, 1)
        self.n += 1

    def settle(self):
        self.eng.wait_ge(self.sem, self.n)

    def link(self, ins):
        self.step(ins)
        self.settle()


def program(nc, x, adj, L0_W, L0_b, Wqkv, bqkv, Wo, bo, ln1_g, ln1_b, W1, b1, W2, b2, ln2_g, ln2_b, out):
    h_table = nc.dram_tensor("h_table", [N + 1, C], fp32).ap()
    h_rows = nc.dram_tensor("h_rows", [B, N, C], fp32).ap()
    lists = nc.dram_tensor("neighbour_lists", [N, LW], i32).ap()
    pooled = nc.dram_tensor("pooled_rows", [N, C], fp32).ap()
    parts_d = nc.dram_tensor("qk_parts", [3 * 2 * C, N], bf16).ap()

    ctx = ExitStack()
    with ctx:
        def sb(name, shape, dt=fp32):
            return ctx.enter_context(nc.sbuf_tensor(name, shape, dt))

        sem_ids = []

        def sem(name):
            s = ctx.enter_context(nc.semaphore(name))
            sem_ids.append(s.num)
            return s

        identf = sb("identf", [P, P])
        identb = sb("identb", [P, P], bf16)
        negident = sb("negident", [P, P], bf16)
        before = sb("before", [P, P], bf16)
        onesb = sb("onesb", [P, P], bf16)
        head_sum = sb("head_sum", [P, HEADS], bf16)
        prio_i = sb("prio_i", [P, N], i32)
        prio = prio_i[:, :].bitcast(fp32)
        node_i = sb("node_i", [P, T], i32)
        level_i = sb("level_i", [P, COUNT], i32)
        level = sb("level", [P, COUNT])
        w_l0 = sb("w_l0", [P, 2, C])
        wqkvT = sb("wqkvT", [P, 3 * C])
        woT = sb("woT", [P, C])
        w1T = sb("w1T", [P, DFF])
        w2T = sb("w2T", [P, FC, C])
        rows = sb("bias_rows", [P, 8, C])
        L0B, BV, BO, G1, B1R, B2, G2, B2R = range(8)
        bqk = sb("bqk", [P, 2])
        b1c = sb("b1c", [P, FC])

        xh = sb("xh", [P, T, C])
        adj_t = sb("adj_t", [P, 3, N], i32)
        vals = sb("vals", [P, T, LW])
        lst = sb("lst", [P, T, LW], i32)
        rank_i = sb("rank_i", [P, T], i32)
        onehot = sb("onehot", [P, T, COUNT], bf16)
        above = sb("above", [P, T, COUNT], bf16)
        abovesum = sb("abovesum", [P, COUNT], bf16)
        rprod = sb("rprod", [P, T, COUNT])
        cnt = sb("cnt", [P, T])
        full = sb("full", [P, 1 + T])
        crowded = sb("crowded", [1 + T, 1])
        crowded_i = sb("crowded_i", [1 + T, 1], i32)
        cand = sb("cand", [P, T, CHUNKS * 8])
        left = sb("left", [P, CHUNKS * 8])
        st1 = sb("st1", [P, T, 6]); mv1 = sb("mv1", [P, T, 2]); nw1 = sb("nw1", [P, 5, T])
        st2 = sb("st2", [P, T, 6]); mv2 = sb("mv2", [P, T, 2]); nw2 = sb("nw2", [P, 5, T])
        nw3 = sb("nw3", [P, 5, T])
        lsorted = sb("lsorted", [P, T, LW], i32)
        nb = sb("nb", [P, 2, S, C])
        agg = sb("agg", [P, 2, C])
        x1 = sb("x1", [P, T, C])
        h2 = sb("h2", [P, T, C])
        x1p = sb("x1p", [P, T, C])
        qs = sb("qs", [P, HEADS, N], bf16)
        ks = sb("ks", [P, HEADS, N], bf16)
        va = sb("va", [P, T, HEADS, SPAN])
        m1 = sb("m1", [P, T, N], bf16)
        barred = sb("barred", [P, T, N], bf16)
        ctx_raw = sb("ctx_raw", [P, HALF])
        rden = sb("rden", [P, TH, GROUP])
        ctxn = sb("ctxn", [P, T, C])
        shift = sb("shift", [P, HEADS * T])
        shf = sb("shf", [HEADS * T, P])
        shr = sb("shr", [HEADS * T, P])
        shp = sb("shp", [HEADS * T, 3, P], bf16)
        nrm = sb("nrm", [HEADS, 4])
        nflag = sb("nflag", [1, 2])
        nflag_i = sb("nflag_i", [1, 1], i32)

        region = sb("region", [P, 12288])

        def view(at, shape):
            n = 1
            for k in shape:
                n *= k
            v = region[:, at:at + n]
            if len(shape) == 2:
                v = v.rearrange("p (a b) -> p a b", a=shape[0])
            return v
        turned = view(0, [N])
        y2 = view(0, [T, C])
        y = view(1024, [T, C])
        hid = view(2048, [FC, HALF])
        hl = view(4096, [T, C])
        h2T = view(4096, [N])
        sq = region[:, 4096:5120].bitcast(bf16).rearrange("p (a n) -> p a n", a=2)
        hT = view(5120, [N])
        aT = view(6144, [N])
        resid = view(5120, [2, N])
        ag = view(7168, [T, C])
        qkf = view(7168, [2, N])
        parts = region[:, 9216:12288].bitcast(bf16).rearrange("p (j a n) -> p j a n", j=3, a=2)
        keys = view(0, [T, N])
        probs = region[:, 8192:12288].rearrange("p (j a n) -> p j a n", j=4, a=2)
        wstage = region[:, 0:2048]

        sc = ctx.enter_context(nc.psum_tensor("sc", [P, 4, HALF], fp32))
        cb = ctx.enter_context(nc.psum_tensor("cb", [P, 2, HALF], fp32))
        ax = ctx.enter_context(nc.psum_tensor("ax", [P, 2, HALF], fp32))
        ax0, ax1 = ax[:, 0, :], ax[:, 1, :]

        s_w_in = sem("w_in")
        s_const_done = sem("const_done")
        s_wT_ready = sem("wT_ready")
        s_wT_used = sem("wT_used")
        s_setup_dve = sem("setup_dve")
        s_zero_out = sem("zero_out")
        s_dve_chain = sem("dve_chain")
        s_x_in = sem("x_in")
        s_rstd1 = sem("rstd1")
        s_h_ready = sem("h_ready")
        s_h_rows_out = sem("h_rows_out")
        s_h_table_out = sem("h_table_out")
        s_adj_in0 = sem("adj_in0")
        s_adj_in1 = sem("adj_in1")
        s_adj_in2 = sem("adj_in2")
        s_adj_used = sem("adj_used")
        s_m1_ready = sem("m1_ready")
        s_full_ready = sem("full_ready")
        s_full_rows = sem("full_rows")
        s_crowded = sem("crowded")
        s_rank_in = sem("rank_in")
        s_rank_counts = sem("rank_counts")
        s_ranks = sem("ranks")
        s_lists_out = sem("lists_out")
        s_lists_in = sem("lists_in")
        s_pool0 = sem("pool0")
        s_pool1 = sem("pool1")
        s_pool2 = sem("pool2")
        s_pool3 = sem("pool3")
        s_pool4 = sem("pool4")
        s_pool5 = sem("pool5")
        s_pool6 = sem("pool6")
        s_pool7 = sem("pool7")
        s_pooled_ready = sem("pooled_ready")
        s_pooled_out0 = sem("pooled_out0")
        s_pooled_out1 = sem("pooled_out1")
        s_nb_used = sem("nb_used")
        s_hl_in = sem("hl_in")
        s_ag_in = sem("ag_in")
        s_x1_in = sem("x1_in")
        s_hT_ready = sem("hT_ready")
        s_hT_sb = sem("hT_sb")
        s_aT_ready = sem("aT_ready")
        s_aT_sb = sem("aT_sb")
        s_lin_ready = sem("lin_ready")
        s_rstd2 = sem("rstd2")
        s_h2_near = sem("h2_near")
        s_h2_far = sem("h2_far")
        s_h2T_ready = sem("h2T_ready")
        s_h2T_sb = sem("h2T_sb")
        s_q_ready = sem("q_ready")
        s_k_ready = sem("k_ready")
        s_v_ready = sem("v_ready")
        s_qk_f = sem("qk_f")
        s_part_ready = sem("part_ready")
        s_parts_out0 = sem("parts_out0")
        s_parts_out1 = sem("parts_out1")
        s_parts_out2 = sem("parts_out2")
        s_qk_in0 = sem("qk_in0")
        s_qk_in1 = sem("qk_in1")
        s_v_sb = sem("v_sb")
        s_sq_ready = sem("sq_ready")
        s_norms_ready = sem("norms_ready")
        s_norms_max = sem("norms_max")
        s_norm_row = sem("norm_row")
        s_nflag_ready = sem("nflag_ready")
        s_gscores = sem("gscores")
        s_gmax = sem("gmax")
        s_gshift = sem("gshift")
        s_gshift_row = sem("gshift_row")
        s_gshift_parts = sem("gshift_parts")
        s_shift_in = sem("shift_in")
        s_scores_ready = sem("scores_ready")
        s_probs_ready = sem("probs_ready")
        s_pv_done = sem("pv_done")
        s_ctx_sb = sem("ctx_sb")
        s_ctxT_raw = sem("ctxT_raw")
        s_ctxn_ready = sem("ctxn_ready")
        s_bar_counts = sem("bar_counts")
        s_bar_ready = sem("bar_ready")
        s_ctxT_ready = sem("ctxT_ready")
        s_ctxT_sb = sem("ctxT_sb")
        s_proj_ready = sem("proj_ready")
        s_rstd3 = sem("rstd3")
        s_z_ready = sem("z_ready")
        s_zT_ready = sem("zT_ready")
        s_zT_sb = sem("zT_sb")
        s_hid_ready = sem("hid_ready")
        s_hid_sb = sem("hid_sb")
        s_ffn_ready = sem("ffn_ready")
        s_ffn_used = sem("ffn_used")
        s_late_counts = sem("late_counts")
        s_late_ready = sem("late_ready")
        s_kept = sem("kept")
        s_rstd4 = sem("rstd4")
        s_out_ready = sem("out_ready")
        s_out_stored = sem("out_stored")
        sem_range = range(min(sem_ids), max(sem_ids) + 1)
        assert len(sem_range) == len(sem_ids)

        def clear_semaphores():
            nc.gpsimd.dma_reset()
            nc.gpsimd.sem_clear(sem_range)
            nc.all_engine_barrier()

        with nc.Block() as block:
            @block.sync
            def _(sp):
                sp.dma_start(w_l0[:, :, :], L0_W.rearrange("(a p) o -> p a o", p=P)).then_inc(s_w_in, 16)
                for j in range(3):
                    sp.dma_start(wstage[:, j * C:(j + 1) * C], Wqkv[j * C:(j + 1) * C, :]).then_inc(s_w_in, 16)
                sp.dma_start(wstage[:, 3 * C:4 * C], Wo[:, :]).then_inc(s_w_in, 16)
                for j in range(FC):
                    sp.dma_start(wstage[:, (4 + j) * C:(5 + j) * C], W1[j * C:(j + 1) * C, :]).then_inc(s_w_in, 16)
                sp.dma_start(wstage[:, 8 * C:12 * C], W2[:, :]).then_inc(s_w_in, 16)
                for j, v in ((L0B, L0_b), (BO, bo), (G1, ln1_g), (B1R, ln1_b), (B2, b2), (G2, ln2_g), (B2R, ln2_b)):
                    sp.dma_start(rows[:, j, :], v.rearrange("(a n) -> a n", a=1).to_broadcast([P, C])).then_inc(s_w_in, 16)
                sp.dma_start(rows[:, BV, :], bqkv[2 * C:3 * C].rearrange("(a n) -> a n", a=1).to_broadcast([P, C])).then_inc(s_w_in, 16)
                for j in range(2):
                    sp.dma_start(bqk[:, j:j + 1], bqkv[j * C:(j + 1) * C].rearrange("(p a) -> p a", a=1)).then_inc(s_w_in, 16)
                for j in range(FC):
                    sp.dma_start(b1c[:, j:j + 1], b1[j * C:(j + 1) * C].rearrange("(p a) -> p a", a=1)).then_inc(s_w_in, 16)
                sp.wait_ge(s_const_done, 1)
                sp.dma_start(h_table[N:N + 1, :], xh[0:1, 0, :]).then_inc(s_zero_out, 16)
                sp.wait_ge(s_zero_out, 16)
                sp.wait_ge(s_w_in, 16 * (1 + 3 + 1 + FC + 1 + 8 + 2 + FC))

            @block.gpsimd
            def _(pool):
                pool.memset(identf[:, :], 0.0)
                pool.memset(identb[:, :], 0.0)
                pool.memset(negident[:, :], 0.0)
                pool.memset(onesb[:, :], 1.0)
                pool.memset(before[:, :], 1.0)
                pool.memset(head_sum[:, :], 1.0).then_inc(s_setup_dve, 1)
                pool.wait_ge(s_setup_dve, 1)
                for m, v in ((identf, 1.0), (identb, 1.0), (negident, MASKED)):
                    pool.affine_select(out=m[:, :], in_=m[:, :], compare_op=ALU.not_equal, fill=v, base=0,
                                       pattern=[[-1, P]], channel_multiplier=1)
                pool.affine_select(out=before[:, :], in_=before[:, :], compare_op=ALU.is_gt, fill=0.0, base=0,
                                   pattern=[[1, P]], channel_multiplier=-1)
                pool.affine_select(out=head_sum[:, :], in_=head_sum[:, :], compare_op=ALU.is_ge, fill=0.0, base=0,
                                   pattern=[[-D, HEADS]], channel_multiplier=1).then_inc(s_setup_dve, 1)
                pool.wait_ge(s_setup_dve, 2)
                pool.affine_select(out=head_sum[:, :], in_=head_sum[:, :], compare_op=ALU.is_ge, fill=0.0, base=D - 1,
                                   pattern=[[D, HEADS]], channel_multiplier=-1)
                pool.iota(prio_i[:, :], pattern=[[-1, N]], base=N, channel_multiplier=0)
                pool.iota(node_i[:, :], pattern=[[P, T]], base=0, channel_multiplier=1)
                pool.iota(level_i[:, :], pattern=[[1, COUNT]], base=0, channel_multiplier=0).then_inc(s_setup_dve, 1)

            @block.vector
            def _(dve):
                nc.vector.memset(xh[:, 0, :], 0.0).then_inc(s_const_done, 1)
                nc.vector.memset(qs[96:128, :, :].rearrange("p h n -> p (h n)").bitcast(i32), 0)
                nc.vector.memset(ks[96:128, :, :], 1.0)
                nc.vector.memset(va[:, :, :, :], 1.0)
                nc.vector.memset(vals[:, :, :], 0.0)
                nc.vector.memset(lst[:, :, :], 0)
                nc.vector.memset(shift[:, :], 0.0)
                dve.wait_ge(s_setup_dve, 3)
                nc.vector.tensor_copy(prio, prio_i[:, :])
                nc.vector.tensor_copy(level[:, :], level_i[:, :])
                for g in range(3):
                    dve.wait_ge(s_wT_ready, g + 1)
                    if g == 0:
                        nc.vector.tensor_copy(wqkvT[:, :], sc[:, 0, 0:3 * C])
                        nc.vector.tensor_copy(woT[:, :], sc[:, 0, 3 * C:4 * C])
                    elif g == 1:
                        nc.vector.tensor_copy(w1T[:, :], sc[:, 1, :])
                    else:
                        nc.vector.tensor_copy(w2T[:, :, :], sc[:, 2, :].rearrange("p (c o) -> p c o", c=FC))

            @block.tensor
            def _(pe):
                pe.wait_ge(s_setup_dve, 2)
                pe.wait_ge(s_w_in, 16 * (1 + 3 + 1 + FC + 1 + 8 + 2 + FC))
                for g in range(3):
                    for j in range(4):
                        k = 4 * g + j
                        last = nc.tensor.transpose(sc[:, g, j * C:(j + 1) * C], wstage[:, k * C:(k + 1) * C], identf[:, :])
                    last.then_inc(s_wT_ready, 1)
        clear_semaphores()

        def rows_of(t):
            return t[0:N, :].rearrange("(t p) c -> p t c", p=P)

        def row_stats(ch, src, st, mv, w, done):
            for t in range(T):
                ch.step(nc.vector.bn_stats(st[:, t, :], src[:, t, :]))
            ch.settle()
            for t in range(T):
                ch.step(nc.vector.bn_aggr(mv[:, t, :], st[:, t, :]))
            ch.settle()
            v = mv[:, :, 1]
            ch.step(nc.vector.tensor_scalar(w[:, 0, :], v, EPS, None, ALU.add))
            ch.link(nc.vector.tensor_scalar(w[:, 1, :], v, EPS, 0.5, ALU.add, ALU.mult))
            ch.link(nc.vector.tensor_scalar(w[:, 3, :].bitcast(i32), w[:, 0, :].bitcast(i32), 1, None,
                                            ALU.logical_shift_right))
            ch.link(nc.vector.tensor_scalar(w[:, 2, :].bitcast(i32), w[:, 3, :].bitcast(i32), -1.0, MAGIC,
                                            ALU.mult, ALU.add))
            for _ in range(3):
                ch.link(nc.vector.tensor_tensor(w[:, 3, :], w[:, 2, :], w[:, 2, :], ALU.mult))
                ch.link(nc.vector.tensor_tensor(w[:, 3, :], w[:, 3, :], w[:, 1, :], ALU.mult))
                ch.link(nc.vector.scalar_tensor_tensor(out=w[:, 2, :], in0=w[:, 3, :], scalar=1.5, in1=w[:, 2, :],
                                                       op0=ALU.subtract, op1=ALU.mult))
            ch.step(nc.vector.tensor_scalar(w[:, 4, :], w[:, 2, :], -1.0, None, ALU.mult))
            nc.vector.tensor_tensor(w[:, 3, :], mv[:, :, 0], w[:, 2, :], ALU.mult).then_inc(done, 1)

        def slot(s, first, pooling, main, post):
            block_ctx = nc.Block()
            block = block_ctx.__enter__()

            OUT = [s_pooled_out0, s_pooled_out1]
            ADJ = [s_adj_in0, s_adj_in1, s_adj_in2]
            POOL = [s_pool0, s_pool1, s_pool2, s_pool3, s_pool4, s_pool5, s_pool6, s_pool7]
            PARTS_OUT = [s_parts_out0, s_parts_out1, s_parts_out2]
            QK_IN = [s_qk_in0, s_qk_in1]
            QK_LOADS = 2 * len(Q_PART) * 16
            order = []
            for t in range(T):
                if pooling:
                    order.append(("mask", t))
                if first:
                    order.append(("list", t))
            slot_of = {o: i for i, o in enumerate(order)}

            @block.sync
            def _(sp):
                def graph(t, b):
                    return t[bass.ds(b, 1), :, :].rearrange("a (t p) c -> p (a t) c", p=P)

                if main:
                    sp.dma_start(hl, graph(h_rows, s)).then_inc(s_hl_in, 16)
                    sp.dma_start(ag, rows_of(pooled)).then_inc(s_ag_in, 16)
                if pooling:
                    sp.dma_start(lsorted[:, :, :], rows_of(lists)).then_inc(s_lists_in, 16)
                if main:
                    sp.dma_start(x1[:, :, :], graph(x, s)).then_inc(s_x1_in, 16)
                if first:
                    sp.dma_start(xh[:, :, :], graph(x, s + 2)).then_inc(s_x_in, 16)

                def load_adj(i):
                    kind, t = order[i]
                    b = s + 2 if kind == "list" else s + 1
                    if i >= 3:
                        sp.wait_ge(s_adj_used, i - 2)
                    sp.dma_start(adj_t[:, i % 3, :], adj[bass.ds(b, 1), t * P:(t + 1) * P, :].rearrange("a p n -> p (a n)")).then_inc(ADJ[i % 3], 16)
                for i in range(min(3, len(order))):
                    load_adj(i)
                if main:
                    for j in range(3):
                        sp.wait_ge(s_part_ready, (4, 5, 6)[j])
                        sp.dma_start(parts_d[j * 2 * C:(j + 1) * 2 * C, :].rearrange("(a p) n -> p a n", p=P), parts[:, j, :, :]).then_inc(PARTS_OUT[j], 16)
                    for g in range(2):
                        for j in range(3):
                            if g == 0:
                                sp.wait_ge(PARTS_OUT[j], 16)
                            for i in range(len(Q_PART)):
                                for a, dst, part in ((0, qs, Q_PART[i]), (1, ks, K_PART[i])):
                                    if part == j:
                                        r = (2 * j + a) * C + g * GROUP * D
                                        sp.dma_start(dst[i * D:(i + 1) * D, g * GROUP:(g + 1) * GROUP, :],
                                                     parts_d[r:r + GROUP * D, :].rearrange("(h d) n -> d h n", d=D)).then_inc(QK_IN[g], 16)
                    sp.wait_ge(s_nflag_ready, 1)
                    wide = sp.value_load(nflag_i[0:1, 0:1], min_val=0, max_val=1)
                    with sp.If(wide > 0):
                        sp.wait_ge(s_gshift_parts, 1)
                        for j in range(3):
                            sp.dma_start(qs[SPLIT + j:SPLIT + j + 1, :, :].rearrange("p h (t n) -> p (h t) n", t=T), shp[:, j, :]).then_inc(s_shift_in, 16)
                if post:
                    sp.wait_ge(s_out_ready, 1)
                    sp.dma_start(graph(out, s - 1), y2).then_inc(s_out_stored, 16)
                for i in range(3, len(order)):
                    load_adj(i)
                if first:
                    sp.wait_ge(s_h_ready, T)
                    sp.dma_start(graph(h_rows, s + 2), xh[:, :, :]).then_inc(s_h_rows_out, 16)
                    if pooling:
                        sp.wait_ge(s_pooled_ready, T)
                    sp.dma_start(rows_of(h_table), xh[:, :, :]).then_inc(s_h_table_out, 16)
                    sp.wait_ge(s_h_rows_out, 16)
                    sp.wait_ge(s_h_table_out, 16)
                if post:
                    sp.wait_ge(s_out_stored, 16)

            @block.gpsimd
            def _(pool):
                def keep():
                    if post:
                        pool.wait_ge(s_out_ready, 1)
                    pool.wait_ge(s_h2_near, TH)
                    nc.gpsimd.tensor_copy(x1p[:, :, :], x1[:, :, :]).then_inc(s_kept, 1)

                if pooling:
                    pool.wait_ge(s_lists_in, 16)
                    if main:
                        pool.wait_ge(s_ag_in, 16)

                    def send(t):
                        pool.wait_ge(s_pooled_ready, t + 1)
                        pool.indirect_dma_start(out=pooled[:, :], out_offset=bass.IndirectOffsetOnAxis(ap=lsorted[:, t, DEST:DEST + 1], axis=0),
                                                in_=agg[:, t % 2, :], in_offset=None).then_inc(OUT[t % 2], 16)
                    for t in range(T):
                        n = pool.value_load(lsorted[0:1, t, COUNT:COUNT + 1], min_val=0, max_val=S)
                        if t >= 2:
                            pool.wait_ge(s_nb_used, t - 1)

                        def gather(lo, hi):
                            for k in range(lo, hi):
                                pool.indirect_dma_start(out=nb[:, t % 2, k, :], out_offset=None, in_=h_table[:, :],
                                                        in_offset=bass.IndirectOffsetOnAxis(ap=lsorted[:, t, k:k + 1], axis=0)).then_inc(POOL[t], 16)
                        gather(0, SIZES[0])
                        for lo, hi in zip(SIZES, SIZES[1:]):
                            with pool.If(n > lo):
                                gather(lo, hi)
                        if t >= 1:
                            send(t - 1)
                        if main and t == T - 2:
                            keep()
                    send(T - 1)
                    pool.wait_ge(s_pooled_out0, 16 * TH)
                    pool.wait_ge(s_pooled_out1, 16 * TH)
                elif main:
                    keep()
                if first:
                    pool.wait_ge(s_ranks, 2)
                    if pooling:
                        pool.wait_ge(s_lists_in, 16)
                    for t in range(T):
                        pool.indirect_dma_start(out=lists[:, :], out_offset=bass.IndirectOffsetOnAxis(ap=rank_i[:, t:t + 1], axis=0),
                                                in_=lst[:, t, :], in_offset=None).then_inc(s_lists_out, 16)
                    pool.wait_ge(s_lists_out, 16 * T)

            @block.vector
            def _(dve):
                ch = Chain(dve, s_dve_chain)

                def row(j):
                    return rows[:, j:j + 1, :].to_broadcast([P, T, C])

                def add_halves(dst, src, j, ready, used):
                    for h in range(2):
                        dve.wait_ge(ready, h + 1)
                        ch.step(nc.vector.tensor_tensor(dst[:, h * TH:(h + 1) * TH, :], src[:, h, :].rearrange("p (t c) -> p t c", t=TH),
                                                        rows[:, j:j + 1, :].to_broadcast([P, TH, C]), ALU.add))
                    ch.settle()
                    if used is not None:
                        dve.sem_inc(used, 1)

                def scaled(v, g):
                    for t in range(T):
                        ch.step(nc.vector.tensor_scalar(v[:, t, :], v[:, t, :], nw3[:, 4, t:t + 1], nw3[:, 3, t:t + 1], ALU.mult, ALU.add))
                    ch.settle()
                    ch.link(nc.vector.tensor_tensor(v, v, row(g), ALU.mult))

                def residual():
                    add_halves(y, cb, BO, s_proj_ready, None)
                    ch.link(nc.vector.scalar_tensor_tensor(out=y, in0=h2[:, :, :], scalar=0.0, in1=y, op0=ALU.max, op1=ALU.add))
                    row_stats(ch, y, st2, mv2, nw3, s_rstd3)
                    dve.wait_ge(s_rstd3, 1)

                def z_rows():
                    scaled(y, G1)
                    nc.vector.tensor_tensor(y, y, row(B1R), ALU.add).then_inc(s_z_ready, 1)
                    dve.wait_ge(s_z_ready, 1)

                def finish():
                    add_halves(y2, ax, B2, s_ffn_ready, s_ffn_used)
                    ch.link(nc.vector.tensor_tensor(y2, y2, y, ALU.add))
                    row_stats(ch, y2, st2, mv2, nw3, s_rstd4)
                    dve.wait_ge(s_rstd4, 1)
                    scaled(y2, G2)
                    ch.link(nc.vector.tensor_tensor(y2, y2, row(B2R), ALU.add))
                    nc.vector.tensor_tensor(y2, y2, x1p[:, :, :], ALU.add).then_inc(s_out_ready, 1)

                def linear():
                    add_halves(h2, sc, L0B, s_lin_ready, None)
                    dve.wait_ge(s_x1_in, 16)
                    ch.link(nc.vector.scalar_tensor_tensor(out=x1[:, :, :], in0=h2[:, :, :], scalar=0.0, in1=x1[:, :, :], op0=ALU.max, op1=ALU.add))
                    row_stats(ch, x1, st2, mv2, nw2, s_rstd2)
                    dve.wait_ge(s_rstd2, 1)
                    for t in range(TH, T):
                        nc.vector.tensor_scalar(h2[:, t, :], x1[:, t, :], nw2[:, 4, t:t + 1], nw2[:, 3, t:t + 1], ALU.mult, ALU.add).then_inc(s_h2_far, 1)

                def qk_parts():
                    dve.wait_ge(s_qk_f, 4)
                    dve.wait_ge(s_part_ready, 4)
                    ch.link(nc.vector.tensor_tensor(resid, qkf, parts[:, 0, :, :], ALU.subtract))
                    nc.vector.tensor_copy(parts[:, 1, :, :], resid).then_inc(s_part_ready, 1)
                    dve.wait_ge(s_part_ready, 5)
                    nc.vector.tensor_tensor(parts[:, 2, :, :], resid, parts[:, 1, :, :], ALU.subtract).then_inc(s_part_ready, 1)
                    bv = rows[:, BV:BV + 1, :].rearrange("p a (h d) -> p a h d", d=D).to_broadcast([P, TH, HEADS, D])
                    for h in range(2):
                        dve.wait_ge(s_v_ready, h + 1)
                        nc.vector.tensor_tensor(va[:, h * TH:(h + 1) * TH, :, 0:D], sc[:, 2 + h, :].rearrange("p (t h d) -> p t h d", t=TH, d=D),
                                                bv, ALU.add).then_inc(s_v_sb, 1)

                def norm_flag():
                    dve.wait_ge(s_norms_ready, 1)
                    ch.link(nc.vector.tensor_reduce(nrm[:, 0:2], sc[0:HEADS, :, :].rearrange("p (a b) n -> p a (b n)", a=2), AX.X, ALU.max))
                    nc.vector.tensor_tensor(nrm[:, 2:3], nrm[:, 0:1], nrm[:, 1:2], ALU.mult).then_inc(s_norms_max, 1)
                    dve.wait_ge(s_norm_row, 1)
                    ch.link(nc.vector.tensor_reduce(nflag[0:1, 0:1], sc[0:1, 0, 0:HEADS], AX.X, ALU.max))
                    nc.vector.tensor_scalar(nflag_i[0:1, 0:1], nflag[0:1, 0:1], SAFE, None, ALU.is_gt).then_inc(s_nflag_ready, 1)
                    dve.wait_ge(s_nflag_ready, 1)
                    return dve.value_load(nflag_i[0:1, 0:1], min_val=0, max_val=1)

                def wide_maxima(wide):
                    with dve.If(wide > 0):
                        for i in range(HEADS * T):
                            dve.wait_ge(s_gscores, i + 1)
                            nc.vector.tensor_reduce(shift[:, i:i + 1], sc[:, 2 * (i % 2):2 * (i % 2) + 2, :].rearrange("p a n -> p (a n)"),
                                                    AX.X, ALU.max).then_inc(s_gmax, 1)
                        dve.wait_ge(s_gmax, HEADS * T)
                        nc.vector.tensor_scalar(shift[:, :], shift[:, :], -1.0, None, ALU.mult).then_inc(s_gshift, 1)
                        dve.wait_ge(s_gshift_row, 1)
                        nc.vector.tensor_copy(shf[:, :], sc[0:HEADS * T, 0, 0:P]).then_inc(s_gshift, 1)
                        dve.wait_ge(s_gshift, 2)
                        nc.vector.tensor_copy(shp[:, 0, :], shf[:, :]).then_inc(s_gshift, 1)
                        dve.wait_ge(s_gshift, 3)
                        nc.vector.tensor_tensor(shr[:, :], shf[:, :], shp[:, 0, :], ALU.subtract).then_inc(s_gshift, 1)
                        dve.wait_ge(s_gshift, 4)
                        nc.vector.tensor_copy(shp[:, 1, :], shr[:, :]).then_inc(s_gshift, 1)
                        dve.wait_ge(s_gshift, 5)
                        nc.vector.tensor_tensor(shp[:, 2, :], shr[:, :], shp[:, 1, :], ALU.subtract).then_inc(s_gshift_parts, 1)

                def adjacency(o):
                    i = slot_of[o]
                    dve.wait_ge(ADJ[i % 3], 16 * (i // 3 + 1))
                    return adj_t[:, i % 3, :]

                def mask_tile(t):
                    a = adjacency(("mask", t))
                    if t == 0 and main:
                        dve.wait_ge(s_late_counts, T)
                    nc.vector.tensor_scalar(m1[:, t, :], a, 0.0, 1.0, ALU.max, ALU.min).then_inc(s_m1_ready, 1)
                    dve.wait_ge(s_m1_ready, t + 1)
                    dve.sem_inc(s_adj_used, 1)

                def list_tile(t):
                    a = adjacency(("list", t))
                    key = keys[:, (t + 1) % T, :]
                    v = vals[:, t, :]
                    if t == T - 1 and post:
                        dve.wait_ge(s_out_stored, 16)
                    nc.vector.scalar_tensor_tensor(out=key, in0=a, scalar=0.0, in1=prio, op0=ALU.not_equal, op1=ALU.mult).then_inc(s_adj_used, 1)
                    dve.wait_ge(s_adj_used, slot_of[("list", t)] + 1)
                    for c in range(CHUNKS):
                        ch.step(nc.vector.max(cand[:, t, 8 * c:8 * c + 8], key[:, c * CW:(c + 1) * CW]))
                    ch.settle()
                    src = cand[:, t, :]
                    for r in range(4):
                        ch.link(nc.vector.max(v[:, 8 * r:8 * r + 8], src))
                        if r < 3:
                            ch.link(nc.vector.match_replace(out=left[:, :], in_to_replace=v[:, 8 * r:8 * r + 8], in_values=src, imm_value=0.0))
                            src = left[:, :]

                def pool_tile(t):
                    if t == 0:
                        dve.wait_ge(s_lists_in, 16)
                    n = dve.value_load(lsorted[0:1, t, COUNT:COUNT + 1], min_val=0, max_val=S)
                    if t >= 2:
                        dve.wait_ge(OUT[t % 2], 16 * (t // 2))
                    for j, m in enumerate(SIZES):
                        low = SIZES[j - 1] if j else -1
                        with dve.If(n > low):
                            with dve.If(n < (m + 1)):
                                dve.wait_ge(POOL[t], 16 * m)
                                nc.vector.tensor_reduce(agg[:, t % 2, :], nb[:, t % 2, 0:m, :].rearrange("p k c -> p c k"), AX.X, ALU.max).then_inc(s_pooled_ready, 1)
                    dve.wait_ge(s_pooled_ready, t + 1)
                    dve.sem_inc(s_nb_used, 1)

                def find_crowded():
                    eighth = cand[:, :, :].rearrange("p t (c k) -> p t c k", k=8)[:, :, :, 7]
                    ch.link(nc.vector.tensor_reduce(full[:, 1:1 + T], eighth, AX.X, ALU.max))
                    nc.vector.tensor_reduce(full[:, 0:1], full[:, 1:1 + T], AX.X, ALU.max).then_inc(s_full_ready, 1)

                def crowded_tiles():
                    dve.wait_ge(s_full_rows, 1)
                    ch.link(nc.vector.tensor_reduce(crowded[:, :], ax0[0:1 + T, 0:P], AX.X, ALU.max))
                    ch.link(nc.vector.tensor_copy(crowded_i[:, :], crowded[:, :]))
                    any_tile = dve.value_load(crowded_i[0:1, 0:1], min_val=0, max_val=N)
                    with dve.If(any_tile > 0):
                        for t in range(T):
                            again = dve.value_load(crowded_i[1 + t:2 + t, 0:1], min_val=0, max_val=N)
                            key = keys[:, (t + 1) % T, :]
                            with dve.If(again > 0):
                                for r in range(4):
                                    v = vals[:, t, 8 * r:8 * r + 8]
                                    nc.vector.max(v, key).then_inc(s_crowded, 1)
                                    dve.wait_ge(s_crowded, 8 * t + 2 * r + 1)
                                    nc.vector.match_replace(out=key, in_to_replace=v, in_values=key, imm_value=0.0).then_inc(s_crowded, 1)
                                    dve.wait_ge(s_crowded, 8 * t + 2 * r + 2)
                            with dve.If(again < 1):
                                dve.sem_inc(s_crowded, 8)

                def make_lists():
                    ch.link(nc.vector.tensor_scalar(rprod[:, :, 0:S], vals[:, :, 0:S], 0.0, None, ALU.is_gt))
                    ch.link(nc.vector.tensor_reduce(cnt[:, :], rprod[:, :, 0:S], AX.X, ALU.add))
                    levels = level[:, :].rearrange("p (a v) -> p a v", a=1).to_broadcast([P, T, COUNT])
                    counts = cnt[:, :].rearrange("p (t a) -> p t a", a=1).to_broadcast([P, T, COUNT])
                    ch.step(nc.vector.tensor_tensor(above[:, :, :], counts, levels, ALU.is_gt))
                    ch.link(nc.vector.tensor_tensor(onehot[:, :, :], counts, levels, ALU.is_equal))
                    ch.link(nc.vector.tensor_reduce(rprod[:, 0, :], above[:, :, :].rearrange("p t v -> p v t"), AX.X, ALU.add))
                    nc.vector.tensor_copy(abovesum[:, :], rprod[:, 0, :]).then_inc(s_rank_in, 1)
                    ch.step(nc.vector.tensor_scalar(lst[:, :, 0:S], vals[:, :, 0:S], -1.0, float(N), ALU.mult, ALU.add))
                    ch.link(nc.vector.tensor_copy(lst[:, :, DEST:DEST + 1], node_i[:, :].rearrange("p (t a) -> p t a", a=1)))
                    nc.vector.tensor_copy(lst[:, :, COUNT:COUNT + 1], cnt[:, :].rearrange("p (t a) -> p t a", a=1)).then_inc(s_ranks, 1)

                def list_ranks():
                    dve.wait_ge(s_rank_counts, 1)
                    dve.wait_ge(s_rank_in, 1)
                    dve.wait_ge(s_ranks, 1)
                    ch.link(nc.vector.tensor_tensor(rprod[:, :, :], ax0[:, 0:T * COUNT].rearrange("p (t v) -> p t v", t=T), onehot[:, :, :], ALU.mult))
                    ch.link(nc.vector.tensor_reduce(cnt[:, :], rprod[:, :, :], AX.X, ALU.add))
                    nc.vector.tensor_copy(rank_i[:, :], cnt[:, :]).then_inc(s_ranks, 1)

                def context(u):
                    qh, g = divmod(u, 2)
                    dve.wait_ge(s_ctxT_raw, u + 1)
                    c = ax0.rearrange("p (t g d) -> p t g d", t=TH, g=GROUP)
                    ch.link(nc.vector.reciprocal(rden[:, :, :], c[:, :, :, D]))
                    r = rden[:, :, :].rearrange("p t (g a) -> p t g a", a=1).to_broadcast([P, TH, GROUP, D])
                    o = ctxn[:, qh * TH:(qh + 1) * TH, g * GROUP * D:(g + 1) * GROUP * D].rearrange("p t (g d) -> p t g d", d=D)
                    nc.vector.tensor_tensor(o, c[:, :, :, 0:D], r, ALU.mult).then_inc(s_ctxn_ready, 1)

                if post:
                    residual()
                if main:
                    linear()
                if post:
                    z_rows()
                if pooling:
                    pool_tile(0)
                if main:
                    qk_parts()
                    wide = norm_flag()
                    wide_maxima(wide)
                if pooling:
                    pool_tile(1)
                if post:
                    finish()
                if pooling:
                    pool_tile(2)
                if first:
                    dve.wait_ge(s_x_in, 16)
                    row_stats(ch, xh, st1, mv1, nw1, s_rstd1)
                if pooling:
                    pool_tile(3)
                for t in range(T):
                    if pooling:
                        mask_tile(t)
                    if first:
                        list_tile(t)
                    if pooling and t in POOL_AFTER:
                        pool_tile(POOL_AFTER[t])
                    if main and t in CONTEXT_AFTER:
                        context(CONTEXT_AFTER[t])
                if first:
                    find_crowded()
                    crowded_tiles()
                    make_lists()
                    list_ranks()
                if main:
                    context(2)
                if main:
                    context(3)
                    with dve.If(wide > 0):
                        nc.vector.memset(qs[96:128, :, :].rearrange("p h n -> p (h n)").bitcast(i32), 0)

            @block.scalar
            def _(act):
                def norm(dst, src, func, w, t, done):
                    nc.scalar.activation(dst[:, t, :], src[:, t, :], func, bias=w[:, 3, t:t + 1], scale=w[:, 4, t:t + 1]).then_inc(done, 1)

                def halves_out(dst, src, ready, done, func=ACT.Copy):
                    for h in range(2):
                        act.wait_ge(ready, h + 1)
                        nc.scalar.activation(dst[:, h * HALF:(h + 1) * HALF], src[:, h, :], func).then_inc(done, 1)

                def late_tile(kt):
                    act.wait_ge(s_late_counts, kt + 1)
                    nc.scalar.activation(barred[:, kt, HALF:N], cb[:, kt % 2, :], ACT.Relu, bias=1.0, scale=-1.0).then_inc(s_late_ready, 1)

                def bar_tile(kt):
                    act.wait_ge(s_bar_counts, kt + 1)
                    nc.scalar.activation(barred[:, kt, 0:HALF], ax1, ACT.Relu, bias=1.0, scale=-1.0).then_inc(s_bar_ready, 1)

                def first_norm():
                    act.wait_ge(s_rstd1, 1)
                    for t in range(T):
                        norm(xh, xh, ACT.Relu, nw1, t, s_h_ready)

                if post:
                    halves_out(turned, sc, s_ctxT_ready, s_ctxT_sb)
                if main:
                    halves_out(hT, sc[:, 2:4, :], s_hT_ready, s_hT_sb)
                    halves_out(aT, ax, s_aT_ready, s_aT_sb)
                    for kt in range(T):
                        late_tile(kt)
                    act.wait_ge(s_rstd2, 1)
                    for t in range(TH):
                        norm(h2, x1, ACT.Identity, nw2, t, s_h2_near)
                    halves_out(h2T, sc[:, 2:4, :], s_h2T_ready, s_h2T_sb, ACT.Relu)
                    for a, ready, bank in ((0, s_q_ready, ax), (1, s_k_ready, sc)):
                        for h in range(2):
                            act.wait_ge(ready, h + 1)
                            cols = slice(h * HALF, (h + 1) * HALF)
                            nc.scalar.activation(qkf[:, a, cols], bank[:, h, :], ACT.Identity, bias=bqk[:, a:a + 1]).then_inc(s_qk_f, 1)
                            nc.scalar.activation(parts[:, 0, a, cols], bank[:, h, :], ACT.Identity, bias=bqk[:, a:a + 1]).then_inc(s_part_ready, 1)
                    act.wait_ge(s_qk_f, 4)
                    act.wait_ge(s_v_ready, 2)
                    nc.scalar.activation(sq, qkf, ACT.Square).then_inc(s_sq_ready, 1)

                def hidden(i):
                    h, c = divmod(i, FC)
                    act.wait_ge(s_hid_ready, i + 1)
                    if h == 1:
                        act.wait_ge(s_ffn_ready, 1)
                    nc.scalar.activation(hid[:, c, :], cb[:, i % 2, :], ACT.Relu, bias=b1c[:, c:c + 1]).then_inc(s_hid_sb, 1)

                if post:
                    halves_out(turned, cb, s_zT_ready, s_zT_sb)
                    for i in range(2 * FC):
                        hidden(i)
                if main:
                    for u in range(UNITS):
                        for j in range(PAIRS):
                            i = u * PAIRS + j
                            act.wait_ge(s_scores_ready, i + 1)
                            if i >= 4:
                                act.wait_ge(s_pv_done, (i - 4) // 2 + 1)
                            nc.scalar.activation(probs[:, i % 4, :, :], sc[:, 2 * (i % 2):2 * (i % 2) + 2, :], ACT.Exp, scale=SCALE).then_inc(s_probs_ready, 1)
                            if u >= 1 and j == 3:
                                if u >= 2:
                                    act.wait_ge(s_ctxT_raw, u - 1)
                                act.wait_ge(s_pv_done, u * T)
                                nc.scalar.activation(ctx_raw[:, :], cb[:, (u - 1) % 2, :], ACT.Copy).then_inc(s_ctx_sb, 1)
                            if first and i == FIRST_NORM_AT:
                                first_norm()
                            if pooling and u >= 2 and j % 4 == 2:
                                bar_tile((u - 2) * 4 + j // 4)
                    act.wait_ge(s_ctxT_raw, 3)
                    act.wait_ge(s_pv_done, UNITS * T)
                    nc.scalar.activation(ctx_raw[:, :], cb[:, 1, :], ACT.Copy).then_inc(s_ctx_sb, 1)
                else:
                    if first:
                        first_norm()
                    if pooling:
                        for kt in range(T):
                            bar_tile(kt)

            @block.tensor
            def _(pe):
                def transposes(dst, src, h, done):
                    for t in range(TH):
                        last = nc.tensor.transpose(dst[:, t * C:(t + 1) * C], src[:, h * TH + t, :], identf[:, :])
                    last.then_inc(done, 1)

                def count_edges(o, half, kt, done):
                    nc.tensor.matmul(o, identb[:, :], m1[:, kt, half * HALF:(half + 1) * HALF], start=True, stop=False)
                    if kt // TH == half:
                        a = kt % TH * P
                        nc.tensor.matmul(o[:, a:a + P], identb[:, :], identb[:, :], start=False, stop=False)
                    for j in range(TH):
                        last = nc.tensor.matmul(o[:, j * P:(j + 1) * P], m1[:, half * TH + j, kt * P:(kt + 1) * P], identb[:, :],
                                                start=False, stop=(j == TH - 1))
                    last.then_inc(done, 1)

                def bar_counts(kt):
                    pe.wait_ge(s_m1_ready, max(kt + 1, TH))
                    if kt:
                        pe.wait_ge(s_bar_ready, kt)
                    elif main and post:
                        pe.wait_ge(s_ffn_used, 1)
                    count_edges(ax1, 0, kt, s_bar_counts)

                def late_counts(kt):
                    if kt >= 2:
                        pe.wait_ge(s_late_ready, kt - 1)
                    elif post:
                        pe.wait_ge(s_rstd3, 1)
                    count_edges(cb[:, kt % 2, :], 1, kt, s_late_counts)

                def full_rows():
                    pe.wait_ge(s_full_ready, 1)
                    if main:
                        pe.wait_ge(s_ctxn_ready, 2)
                    nc.tensor.transpose(ax0[0:1 + T, 0:P], full[:, :], identf[:, :]).then_inc(s_full_rows, 1)

                def rank_counts():
                    pe.wait_ge(s_rank_in, 1)
                    for t in range(T):
                        o = ax0[:, t * COUNT:(t + 1) * COUNT]
                        nc.tensor.matmul(o, onesb[:, :], abovesum[:, :], start=True, stop=False)
                        for e in range(t):
                            nc.tensor.matmul(o, onesb[:, :], onehot[:, e, :], start=False, stop=False)
                        last = nc.tensor.matmul(o, before[:, :], onehot[:, t, :], start=False, stop=True)
                    last.then_inc(s_rank_counts, 1)

                def scores(i):
                    u, j = divmod(i, PAIRS)
                    qh, g = divmod(u, 2)
                    kt, pair = divmod(j, 2)
                    if i >= 2:
                        pe.wait_ge(s_probs_ready, i - 1)
                    if i == PAIRS:
                        pe.wait_ge(s_qk_in1, QK_LOADS)
                    q = slice(qh * HALF, (qh + 1) * HALF)
                    for a in range(2):
                        h = g * GROUP + pair * 2 + a
                        o = sc[:, 2 * (i % 2) + a, :]
                        nc.tensor.matmul(o, ks[0:SPLIT + SHIFT, h, kt * P:(kt + 1) * P], qs[0:SPLIT + SHIFT, h, q], start=True, stop=False)
                    for a in range(2):
                        o = sc[:, 2 * (i % 2) + a, :]
                        last = nc.tensor.matmul(o, negident[:, :], barred[:, kt, q], start=False, stop=True)
                    last.then_inc(s_scores_ready, 1)

                def contexts(i):
                    u, kt = divmod(i, T)
                    g = u % 2
                    if kt == 0 and u >= 2:
                        pe.wait_ge(s_ctx_sb, u - 1)
                    pe.wait_ge(s_probs_ready, 2 * i + 2)
                    for a in range(GROUP):
                        last = nc.tensor.matmul(cb[SPAN * a:SPAN * (a + 1), u % 2, :], va[:, kt, g * GROUP + a, :],
                                                probs[:, (2 * i + a // 2) % 4, a % 2, :], start=(kt == 0), stop=(kt == T - 1))
                    last.then_inc(s_pv_done, 1)

                def context_rows(u):
                    pe.wait_ge(s_ctx_sb, u + 1)
                    if u:
                        pe.wait_ge(s_ctxn_ready, u)
                    elif post:
                        pe.wait_ge(s_ffn_used, 1)
                    if u == 2 and first:
                        pe.wait_ge(s_ranks, 2)
                    for t in range(TH):
                        last = nc.tensor.transpose(ax0[:, t * P:(t + 1) * P], ctx_raw[:, t * P:(t + 1) * P], identf[:, :])
                    last.then_inc(s_ctxT_raw, 1)

                def hidden(i):
                    h, c = divmod(i, FC)
                    if i >= 2:
                        pe.wait_ge(s_hid_sb, i - 1)
                    else:
                        pe.wait_ge(s_zT_sb, 2)
                    nc.tensor.matmul(cb[:, i % 2, :], w1T[:, c * P:(c + 1) * P], turned[:, h * HALF:(h + 1) * HALF], start=True, stop=True).then_inc(s_hid_ready, 1)

                def forward(h):
                    pe.wait_ge(s_hid_sb, (h + 1) * FC)
                    if main:
                        pe.wait_ge(s_part_ready, 2)
                    for t in range(TH):
                        for c in range(FC):
                            last = nc.tensor.matmul(ax[:, h, t * C:(t + 1) * C], hid[:, c, t * P:(t + 1) * P], w2T[:, c, :], start=(c == 0), stop=(c == FC - 1))
                    last.then_inc(s_ffn_ready, 1)

                if post:
                    for h in range(2):
                        transposes(sc[:, h, :], ctxn, h, s_ctxT_ready)
                    pe.wait_ge(s_ctxT_sb, 2)
                    for h in range(2):
                        for t in range(TH):
                            cols = slice((h * TH + t) * P, (h * TH + t + 1) * P)
                            last = nc.tensor.matmul(cb[:, h, t * C:(t + 1) * C], turned[:, cols], woT[:, :], start=True, stop=True)
                        last.then_inc(s_proj_ready, 1)
                if main:
                    pe.wait_ge(s_hl_in, 16)
                    for h in range(2):
                        transposes(sc[:, 2 + h, :], hl, h, s_hT_ready)
                if main:
                    pe.wait_ge(s_ag_in, 16)
                    for h in range(2):
                        transposes(ax[:, h, :], ag, h, s_aT_ready)
                    pe.wait_ge(s_hT_sb, 2)
                    pe.wait_ge(s_aT_sb, 2)
                    for h in range(2):
                        for t in range(TH):
                            cols = slice((h * TH + t) * P, (h * TH + t + 1) * P)
                            o = sc[:, h, t * C:(t + 1) * C]
                            nc.tensor.matmul(o, hT[:, cols], w_l0[:, 0, :], start=True, stop=False)
                            last = nc.tensor.matmul(o, aT[:, cols], w_l0[:, 1, :], start=False, stop=True)
                        last.then_inc(s_lin_ready, 1)
                    for kt in range(T):
                        late_counts(kt)
                    for h in range(2):
                        pe.wait_ge((s_h2_near, s_h2_far)[h], TH)
                        transposes(sc[:, 2 + h, :], h2, h, s_h2T_ready)
                    for h in range(2):
                        pe.wait_ge(s_h2T_sb, h + 1)
                        nc.tensor.matmul(ax[:, h, :], wqkvT[:, 0:C], h2T[:, h * HALF:(h + 1) * HALF], start=True, stop=True).then_inc(s_q_ready, 1)
                    for h in range(2):
                        nc.tensor.matmul(sc[:, h, :], wqkvT[:, C:2 * C], h2T[:, h * HALF:(h + 1) * HALF], start=True, stop=True).then_inc(s_k_ready, 1)
                    for h in range(2):
                        for t in range(TH):
                            cols = slice((h * TH + t) * P, (h * TH + t + 1) * P)
                            last = nc.tensor.matmul(sc[:, 2 + h, t * C:(t + 1) * C], h2T[:, cols], wqkvT[:, 2 * C:3 * C], start=True, stop=True)
                        last.then_inc(s_v_ready, 1)
                if post:
                    pe.wait_ge(s_z_ready, 1)
                    if main:
                        pe.wait_ge(s_late_ready, T)
                    for h in range(2):
                        transposes(cb[:, h, :], y, h, s_zT_ready)
                    for i in range(FC):
                        hidden(i)
                    forward(0)
                if main:
                    pe.wait_ge(s_sq_ready, 1)
                    pe.wait_ge(s_part_ready, 4)
                    pe.wait_ge(s_v_sb, 2)
                    for a in range(2):
                        for h in range(2):
                            last = nc.tensor.matmul(sc[0:HEADS, 2 * a + h, :], head_sum[:, :], sq[:, a, h * HALF:(h + 1) * HALF], start=True, stop=True)
                    last.then_inc(s_norms_ready, 1)
                if post:
                    for i in range(FC, 2 * FC):
                        hidden(i)
                if main:
                    pe.wait_ge(s_norms_max, 1)
                    nc.tensor.transpose(sc[0:1, 0, 0:HEADS], nrm[:, 2:3], identf[0:HEADS, 0:HEADS]).then_inc(s_norm_row, 1)
                if post:
                    forward(1)
                if main:
                    pe.wait_ge(s_qk_in0, QK_LOADS)
                    pe.wait_ge(s_late_ready, T)
                    pe.wait_ge(s_nflag_ready, 1)
                    wide = pe.value_load(nflag_i[0:1, 0:1], min_val=0, max_val=1)
                    with pe.If(wide > 0):
                        pe.wait_ge(s_qk_in1, QK_LOADS)
                        for i in range(HEADS * T):
                            h, qt = divmod(i, T)
                            if i >= 2:
                                pe.wait_ge(s_gmax, i - 1)
                            for a in range(2):
                                nc.tensor.matmul(sc[:, 2 * (i % 2) + a, :], qs[0:SPLIT, h, qt * P:(qt + 1) * P], ks[0:SPLIT, h, a * HALF:(a + 1) * HALF],
                                                 start=True, stop=False)
                                last = nc.tensor.matmul(sc[:, 2 * (i % 2) + a, :], negident[:, :], barred[:, qt, a * HALF:(a + 1) * HALF], start=False, stop=True)
                            last.then_inc(s_gscores, 1)
                        pe.wait_ge(s_gshift, 1)
                        nc.tensor.transpose(sc[0:HEADS * T, 0, 0:P], shift[:, :], identf[:, :]).then_inc(s_gshift_row, 1)
                        pe.wait_ge(s_shift_in, 48)

                    for i in range(UNITS * PAIRS):
                        u, j = divmod(i, PAIRS)
                        scores(i)
                        if i >= 3 and i % 2 == 1:
                            contexts((i - 3) // 2)
                        if u >= 1 and j == ROWS_AT[u]:
                            context_rows(u - 1)
                        if pooling and u >= 2 and j % 4 == 1:
                            bar_counts((u - 2) * 4 + j // 4)
                        if first and i == FULL_AT:
                            full_rows()
                        if first and i == RANKS_AT:
                            rank_counts()
                    contexts(UNITS * T - 1)
                    context_rows(3)
                else:
                    if pooling:
                        for kt in range(T):
                            bar_counts(kt)
                    if first:
                        full_rows()
                        rank_counts()
            block_ctx.__exit__(None, None, None)
            clear_semaphores()

        slot(-2, True, False, False, False)
        slot(-1, True, True, False, False)
        slot(0, True, True, True, False)
        with nc.Fori(0, B - 3) as i:
            slot(i + 1, True, True, True, True)
        slot(B - 2, False, True, True, True)
        slot(B - 1, False, False, True, True)
        slot(B, False, False, False, True)


_INS = ['x', 'adj', 'L0_gnn_W', 'L0_gnn_b', 'L1_gnn_Wqkv', 'L1_gnn_bqkv', 'L1_gnn_Wo', 'L1_gnn_bo', 'L1_gnn_ln1_g', 'L1_gnn_ln1_b',
        'L1_gnn_W1', 'L1_gnn_b1', 'L1_gnn_W2', 'L1_gnn_b2', 'L1_gnn_ln2_g', 'L1_gnn_ln2_b']
_OUTS = [((B, N, C), 'float32')]


def kernel(**inputs):
    import numpy as _np
    import concourse.bacc as _bacc
    from concourse import mybir as _mybir
    from concourse.bass_utils import run_bass_kernel_spmd as _run

    nc = _bacc.Bacc("TRN2", target_bir_lowering=False, num_devices=1)
    arrays, args = {}, []
    for name in _INS:
        a = _np.ascontiguousarray(inputs[name])
        arrays[f"in_{name}_dram"] = a
        args.append(nc.dram_tensor(f"in_{name}_dram", a.shape, _mybir.dt.from_np(a.dtype), kind="ExternalInput").ap())
    for i, (shape, dtype) in enumerate(_OUTS):
        dt = _mybir.dt.from_np(_np.dtype(dtype))
        args.append(nc.dram_tensor(f"out_{i}_dram", shape, dt, kind="ExternalOutput").ap())
    program(nc, *args)
    r = _run(nc, [arrays], core_ids=[0])
    return r.results[0]["out_0_dram"]
```

```python
import concourse.bass as bass
from concourse import mybir
from contextlib import ExitStack

fp32 = mybir.dt.float32
bf16 = mybir.dt.bfloat16
i32 = mybir.dt.int32
ALU = mybir.AluOpType
ACT = mybir.ActivationFunctionType
AX = mybir.AxisListType

B, N, C = 8, 1024, 128
P = 128
T = N // P
HALF = N // 2
TH = T // 2
S = 25
LW = 32
DEST, COUNT = 25, 26
HEADS, D = 8, 16
DFF = 4 * C
FC = DFF // P
EPS = 1e-5
SCALE = 1.0 / D ** 0.5
MASKED = -float(2 ** 100)
GROUP = 4
SPAN = P // GROUP
PAIRS = 2 * T
UNITS = 4
SAFE = (60.0 / SCALE) ** 2
CHUNKS = 8
CW = N // CHUNKS
FINE_SIZES = [6, 8, 10, 12, 18, 25]
SIZES = [8, 12, 16, 20, 25]
Q_PART = [0, 0, 1, 1, 0, 2]
K_PART = [0, 1, 0, 1, 2, 0]
SPLIT = len(Q_PART) * D
SHIFT = 3
MAGIC = float(0x5F3759DF)
CONTEXT_AFTER = {2: 0, 6: 1}
ROWS_AT = {1: 5, 2: 5, 3: 6}
FULL_AT = 49
RANKS_AT = 53
WARM_STATS, WARM_END = 8, 3
NORM_FROM = 12
BARS_FROM = 56
TURN_AT = 57
MASK_EVERY = 4


class Chain:

    def __init__(self, eng, sem):
        self.eng, self.sem, self.n = eng, sem, 0

    def step(self, ins):
        ins.then_inc(self.sem, 1)
        self.n += 1

    def settle(self):
        self.eng.wait_ge(self.sem, self.n)

    def link(self, ins):
        self.step(ins)
        self.settle()


def program(nc, x, adj, L0_W, L0_b, Wqkv, bqkv, Wo, bo, ln1_g, ln1_b, W1, b1, W2, b2, ln2_g, ln2_b, out):
    h_table = nc.dram_tensor("h_table", [N + 1, C], fp32).ap()
    h_rows = nc.dram_tensor("h_rows", [B, N, C], fp32).ap()
    lists = nc.dram_tensor("neighbour_lists", [N, LW], i32).ap()
    pooled = nc.dram_tensor("pooled_rows", [N, C], fp32).ap()
    parts_d = nc.dram_tensor("qk_parts", [3 * 2 * C, N], bf16).ap()

    ctx = ExitStack()
    with ctx:
        def sb(name, shape, dt=fp32):
            return ctx.enter_context(nc.sbuf_tensor(name, shape, dt))

        sem_ids = []

        def sem(name):
            s = ctx.enter_context(nc.semaphore(name))
            sem_ids.append(s.num)
            return s

        identf = sb("identf", [P, P])
        identb = sb("identb", [P, P], bf16)
        negident = sb("negident", [P, P], bf16)
        before = sb("before", [P, P], bf16)
        onesb = sb("onesb", [P, P], bf16)
        ones_row = sb("ones_row", [1, P])
        head_sum = sb("head_sum", [P, HEADS], bf16)
        prio_i = sb("prio_i", [P, N], i32)
        prio = prio_i[:, :].bitcast(fp32)
        node_i = sb("node_i", [P, T], i32)
        level_i = sb("level_i", [P, COUNT], i32)
        level = sb("level", [P, COUNT])
        w_l0 = sb("w_l0", [P, 2, C])
        wqkvT = sb("wqkvT", [P, 3 * C])
        woT = sb("woT", [P, C])
        w1T = sb("w1T", [P, DFF])
        w2T = sb("w2T", [P, FC, C])
        rows = sb("bias_rows", [P, 8, C])
        L0B, BV, BO, G1, B1R, B2, G2, B2R = range(8)
        bqk = sb("bqk", [P, 2])
        b1c = sb("b1c", [P, FC])

        xh = sb("xh", [P, T, C])
        adj_t = sb("adj_t", [P, 2, N], i32)
        adj_m = sb("adj_m", [P, N], i32)
        vals = sb("vals", [P, T, LW])
        lst = sb("lst", [P, T, LW], i32)
        rank_i = sb("rank_i", [P, T], i32)
        onehot = sb("onehot", [P, T, COUNT], bf16)
        above = sb("above", [P, T, COUNT], bf16)
        abovesum = sb("abovesum", [P, COUNT], bf16)
        rprod = sb("rprod", [P, T, COUNT])
        cnt = sb("cnt", [P, T])
        full = sb("full", [P, 1 + T])
        crowded = sb("crowded", [1 + T, 1])
        crowded_i = sb("crowded_i", [1 + T, 1], i32)
        cand = sb("cand", [P, T, CHUNKS * 8])
        left = sb("left", [P, 2, CHUNKS * 8])
        st1 = sb("st1", [P, T, 6]); mv1 = sb("mv1", [P, T, 2]); nw1 = sb("nw1", [P, 5, T])
        st2 = sb("st2", [P, T, 6]); st3 = sb("st3", [P, T, 6])
        mv23 = sb("mv23", [P, 2 * T, 2]); nw23 = sb("nw23", [P, 5, 2 * T])
        mv2, mv3 = mv23[:, 0:T, :], mv23[:, T:2 * T, :]
        nw2, nw3 = nw23[:, :, 0:T], nw23[:, :, T:2 * T]
        lsorted = sb("lsorted", [P, T, LW], i32)
        nb = sb("nb", [P, 2, S, C])
        agg = sb("agg", [P, 2, C])
        x1 = sb("x1", [P, T, C])
        h2 = sb("h2", [P, T, C])
        x1p = sb("x1p", [P, T, C])
        qs = sb("qs", [P, HEADS, N], bf16)
        ks = sb("ks", [P, HEADS, N], bf16)
        va = sb("va", [P, T, HEADS, SPAN])
        m1 = sb("m1", [P, T, N], bf16)
        barred = sb("barred", [P, T, N], bf16)
        ctx_raw = sb("ctx_raw", [P, HALF])
        shr = ctx_raw[0:HEADS * T, 0:P]
        rden = sb("rden", [P, TH, GROUP])
        ctxn = sb("ctxn", [P, T, C])
        shift = sb("shift", [P, HEADS * T])
        shf = sb("shf", [HEADS * T, P])
        shp = sb("shp", [HEADS * T, 3, P], bf16)
        nrm = sb("nrm", [HEADS, 4])
        nflag = sb("nflag", [1, 2])
        nflag_i = sb("nflag_i", [1, 1], i32)

        region = sb("region", [P, 12288])

        def view(at, shape):
            n = 1
            for k in shape:
                n *= k
            v = region[:, at:at + n]
            if len(shape) == 2:
                v = v.rearrange("p (a b) -> p a b", a=shape[0])
            return v
        turned = view(0, [N])
        y2 = view(0, [T, C])
        y = view(1024, [T, C])
        hid = view(2048, [FC, HALF])
        hl = view(4096, [T, C])
        h2T = view(4096, [N])
        sq = region[:, 4096:5120].bitcast(bf16).rearrange("p (a n) -> p a n", a=2)
        hT = view(5120, [N])
        aT = view(6144, [N])
        resid = view(5120, [2, N])
        ag = view(7168, [T, C])
        qkf = view(7168, [2, N])
        parts = region[:, 9216:12288].bitcast(bf16).rearrange("p (j a n) -> p j a n", j=3, a=2)
        keys = view(0, [T, N])
        probs = region[:, 8192:12288].rearrange("p (j a n) -> p j a n", j=4, a=2)
        wstage = region[:, 8192:10240]

        sc = ctx.enter_context(nc.psum_tensor("sc", [P, 4, HALF], fp32))
        cb = ctx.enter_context(nc.psum_tensor("cb", [P, 2, HALF], fp32))
        ax = ctx.enter_context(nc.psum_tensor("ax", [P, 2, HALF], fp32))
        ax0, ax1 = ax[:, 0, :], ax[:, 1, :]

        s_w_in = sem("w_in")
        s_wT_ready = sem("wT_ready")
        s_setup_dve = sem("setup_dve")
        s_zero_out = sem("zero_out")
        s_dve_chain = sem("dve_chain")
        s_x_in = sem("x_in")
        s_rstd1 = sem("rstd1")
        s_h_ready = sem("h_ready")
        s_h_rows_out = sem("h_rows_out")
        s_h_table_out = sem("h_table_out")
        s_adj_in0 = sem("adj_in0")
        s_adj_in1 = sem("adj_in1")
        s_adj_mask_in = sem("adj_mask_in")
        s_adj_used = sem("adj_used")
        s_m1_ready = sem("m1_ready")
        s_full_ready = sem("full_ready")
        s_full_rows = sem("full_rows")
        s_crowded = sem("crowded")
        s_rank_in = sem("rank_in")
        s_rank_counts = sem("rank_counts")
        s_ranks = sem("ranks")
        s_lists_out = sem("lists_out")
        s_lists_in = sem("lists_in")
        s_pool0 = sem("pool0")
        s_pool1 = sem("pool1")
        s_pool2 = sem("pool2")
        s_pool3 = sem("pool3")
        s_pool4 = sem("pool4")
        s_pool5 = sem("pool5")
        s_pool6 = sem("pool6")
        s_pool7 = sem("pool7")
        s_pooled_ready = sem("pooled_ready")
        s_pooled_out0 = sem("pooled_out0")
        s_pooled_out1 = sem("pooled_out1")
        s_nb_used = sem("nb_used")
        s_hl_in = sem("hl_in")
        s_ag_in = sem("ag_in")
        s_x1_in = sem("x1_in")
        s_hT_ready = sem("hT_ready")
        s_hT_sb = sem("hT_sb")
        s_aT_ready = sem("aT_ready")
        s_aT_sb = sem("aT_sb")
        s_lin_ready = sem("lin_ready")
        s_rstd2 = sem("rstd2")
        s_h2_near = sem("h2_near")
        s_h2_far = sem("h2_far")
        s_h2T_ready = sem("h2T_ready")
        s_h2T_sb = sem("h2T_sb")
        s_q_ready = sem("q_ready")
        s_k_ready = sem("k_ready")
        s_v_ready = sem("v_ready")
        s_qk_f = sem("qk_f")
        s_part_ready = sem("part_ready")
        s_mid_ready = sem("mid_ready")
        s_low_ready = sem("low_ready")
        s_parts_out0 = sem("parts_out0")
        s_parts_out1 = sem("parts_out1")
        s_parts_out2 = sem("parts_out2")
        s_qk_in0 = sem("qk_in0")
        s_qk_in1 = sem("qk_in1")
        s_v_sb = sem("v_sb")
        s_sq_ready = sem("sq_ready")
        s_norms_ready = sem("norms_ready")
        s_norms_max = sem("norms_max")
        s_norm_row = sem("norm_row")
        s_nflag_ready = sem("nflag_ready")
        s_gscores = sem("gscores")
        s_gmax = sem("gmax")
        s_gshift = sem("gshift")
        s_gshift_row = sem("gshift_row")
        s_gshift_parts = sem("gshift_parts")
        s_shift_in = sem("shift_in")
        s_scores_ready = sem("scores_ready")
        s_probs_ready = sem("probs_ready")
        s_pv_done = sem("pv_done")
        s_ctx_sb = sem("ctx_sb")
        s_ctxT_raw = sem("ctxT_raw")
        s_ctxn_ready = sem("ctxn_ready")
        s_bar_counts = sem("bar_counts")
        s_bar_ready = sem("bar_ready")
        s_near_turned = sem("near_turned")
        s_near_sb = sem("near_sb")
        s_ctxT_ready = sem("ctxT_ready")
        s_ctxT_sb = sem("ctxT_sb")
        s_proj_ready = sem("proj_ready")
        s_rstd3 = sem("rstd3")
        s_y_filled = sem("y_filled")
        s_z_ready = sem("z_ready")
        s_zT_ready = sem("zT_ready")
        s_zT_sb = sem("zT_sb")
        s_hid_ready = sem("hid_ready")
        s_hid_sb = sem("hid_sb")
        s_ffn_ready = sem("ffn_ready")
        s_ffn_used = sem("ffn_used")
        s_late_counts = sem("late_counts")
        s_late_ready = sem("late_ready")
        s_kept = sem("kept")
        s_rstd4 = sem("rstd4")
        s_out_ready = sem("out_ready")
        s_out_stored = sem("out_stored")
        sem_range = range(min(sem_ids), max(sem_ids) + 1)
        assert len(sem_range) == len(sem_ids)

        def clear_semaphores():
            nc.gpsimd.dma_reset()
            nc.gpsimd.sem_clear(sem_range)
            nc.all_engine_barrier()

        with nc.Block() as block:
            @block.gpsimd
            def _(pool):
                pool.memset(identf[:, :], 0.0)
                pool.memset(identb[:, :], 0.0)
                pool.memset(negident[:, :], 0.0)
                pool.memset(onesb[:, :], 1.0)
                pool.memset(ones_row[:, :], 1.0)
                pool.memset(before[:, :], 1.0)
                pool.memset(head_sum[:, :], 1.0).then_inc(s_setup_dve, 1)
                pool.wait_ge(s_setup_dve, 1)
                for m, v in ((identf, 1.0), (identb, 1.0), (negident, MASKED)):
                    pool.affine_select(out=m[:, :], in_=m[:, :], compare_op=ALU.not_equal, fill=v, base=0,
                                       pattern=[[-1, P]], channel_multiplier=1)
                pool.affine_select(out=before[:, :], in_=before[:, :], compare_op=ALU.is_gt, fill=0.0, base=0,
                                   pattern=[[1, P]], channel_multiplier=-1)
                pool.affine_select(out=head_sum[:, :], in_=head_sum[:, :], compare_op=ALU.is_ge, fill=0.0, base=0,
                                   pattern=[[-D, HEADS]], channel_multiplier=1).then_inc(s_setup_dve, 1)
                pool.wait_ge(s_setup_dve, 2)
                pool.affine_select(out=head_sum[:, :], in_=head_sum[:, :], compare_op=ALU.is_ge, fill=0.0, base=D - 1,
                                   pattern=[[D, HEADS]], channel_multiplier=-1)
                pool.iota(prio_i[:, :], pattern=[[-1, N]], base=N, channel_multiplier=0)
                pool.iota(node_i[:, :], pattern=[[P, T]], base=0, channel_multiplier=1)
                pool.iota(level_i[:, :], pattern=[[1, COUNT]], base=0, channel_multiplier=0).then_inc(s_setup_dve, 1)

            @block.vector
            def _(dve):
                nc.vector.memset(agg[:, 0, :], 0.0)
                nc.vector.memset(lst[:, :, :], 0)
                dve.wait_ge(s_setup_dve, 3)
                nc.vector.tensor_copy(prio, prio_i[:, :])
                nc.vector.tensor_copy(level[:, :], level_i[:, :])
        clear_semaphores()

        def rows_of(t):
            return t[0:N, :].rearrange("(t p) c -> p t c", p=P)

        def moments(ch, src, st, mv, tiles=(0, T), fill=None):
            for h in range(tiles[0] // TH, tiles[1] // TH):
                if fill is not None:
                    fill(h)
                    ch.settle()
                for t in range(h * TH, (h + 1) * TH):
                    ch.step(nc.vector.bn_stats(st[:, t, :], src[:, t, :]))
            ch.settle()
            for t in range(*tiles):
                ch.step(nc.vector.bn_aggr(mv[:, t, :], st[:, t, :]))
            ch.settle()

        def inverse_roots(ch, mv, w, k, done):
            v = mv[:, k, 1]
            ch.step(nc.vector.tensor_scalar(w[:, 0, k], v, EPS, None, ALU.add))
            ch.link(nc.vector.tensor_scalar(w[:, 1, k], v, EPS, 0.5, ALU.add, ALU.mult))
            ch.link(nc.vector.tensor_scalar(w[:, 3, k].bitcast(i32), w[:, 0, k].bitcast(i32), 1, None,
                                            ALU.logical_shift_right))
            ch.link(nc.vector.tensor_scalar(w[:, 2, k].bitcast(i32), w[:, 3, k].bitcast(i32), -1.0, MAGIC,
                                            ALU.mult, ALU.add))
            for _ in range(3):
                ch.link(nc.vector.tensor_tensor(w[:, 3, k], w[:, 2, k], w[:, 2, k], ALU.mult))
                ch.link(nc.vector.tensor_tensor(w[:, 3, k], w[:, 3, k], w[:, 1, k], ALU.mult))
                ch.link(nc.vector.scalar_tensor_tensor(out=w[:, 2, k], in0=w[:, 3, k], scalar=1.5, in1=w[:, 2, k],
                                                       op0=ALU.subtract, op1=ALU.mult))
            ch.step(nc.vector.tensor_scalar(w[:, 4, k], w[:, 2, k], -1.0, None, ALU.mult))
            nc.vector.tensor_tensor(w[:, 3, k], mv[:, k, 0], w[:, 2, k], ALU.mult).then_inc(done, 1)

        def row_stats(ch, src, st, mv, w, done, tiles=(0, T), fill=None):
            moments(ch, src, st, mv, tiles, fill)
            inverse_roots(ch, mv, w, slice(*tiles), done)

        def slot(s, first, pooling, main, post):
            block_ctx = nc.Block()
            block = block_ctx.__enter__()

            OUT = [s_pooled_out0, s_pooled_out1]
            ADJ = [s_adj_in0, s_adj_in1]
            POOL = [s_pool0, s_pool1, s_pool2, s_pool3, s_pool4, s_pool5, s_pool6, s_pool7]
            PARTS_OUT = [s_parts_out0, s_parts_out1, s_parts_out2]
            sizes = SIZES if main else FINE_SIZES
            pieces = [(0, T)] if main else [(0, TH), (TH, T)]
            zbank, hbank = (cb, cb) if main else (sc[:, 0:2, :], sc[:, 2:4, :])

            def hid_bank(i):
                return sc[:, i - 2, :] if main and i in (2, 3) else hbank[:, i % 2, :]
            QK_IN = [s_qk_in0, s_qk_in1]
            QK_LOADS = 2 * len(Q_PART) * 16

            prepare = pooling and not main
            zero_row = first and not pooling
            W_LOADS = 16 * (1 + 3 + 1 + FC + 1 + 8 + 2 + FC)

            @block.sync
            def _(sp):
                def load_weights():
                    sp.dma_start(w_l0[:, :, :], L0_W.rearrange("(a p) o -> p a o", p=P)).then_inc(s_w_in, 16)
                    for j in range(3):
                        sp.dma_start(wstage[:, j * C:(j + 1) * C], Wqkv[j * C:(j + 1) * C, :]).then_inc(s_w_in, 16)
                    sp.dma_start(wstage[:, 3 * C:4 * C], Wo[:, :]).then_inc(s_w_in, 16)
                    for j in range(FC):
                        sp.dma_start(wstage[:, (4 + j) * C:(5 + j) * C], W1[j * C:(j + 1) * C, :]).then_inc(s_w_in, 16)
                    sp.dma_start(wstage[:, 8 * C:12 * C], W2[:, :]).then_inc(s_w_in, 16)
                    for j, v in ((L0B, L0_b), (BO, bo), (G1, ln1_g), (B1R, ln1_b), (B2, b2), (G2, ln2_g), (B2R, ln2_b)):
                        sp.dma_start(rows[:, j, :], v.rearrange("(a n) -> a n", a=1).to_broadcast([P, C])).then_inc(s_w_in, 16)
                    sp.dma_start(rows[:, BV, :], bqkv[2 * C:3 * C].rearrange("(a n) -> a n", a=1).to_broadcast([P, C])).then_inc(s_w_in, 16)
                    for j in range(2):
                        sp.dma_start(bqk[:, j:j + 1], bqkv[j * C:(j + 1) * C].rearrange("(p a) -> p a", a=1)).then_inc(s_w_in, 16)
                    for j in range(FC):
                        sp.dma_start(b1c[:, j:j + 1], b1[j * C:(j + 1) * C].rearrange("(p a) -> p a", a=1)).then_inc(s_w_in, 16)

                def graph(t, b):
                    return t[bass.ds(b, 1), :, :].rearrange("a (t p) c -> p (a t) c", p=P)

                if main:
                    sp.dma_start(hl, graph(h_rows, s)).then_inc(s_hl_in, 16)
                    sp.dma_start(ag, rows_of(pooled)).then_inc(s_ag_in, 16)
                if pooling:
                    sp.dma_start(lsorted[:, :, :], rows_of(lists)).then_inc(s_lists_in, 16)
                if main:
                    sp.dma_start(x1[:, :, :], graph(x, s)).then_inc(s_x1_in, 16)
                def load_adj(t):
                    if t >= 2:
                        sp.wait_ge(s_adj_used, t - 1)
                    sp.dma_start(adj_t[:, t % 2, :], adj[bass.ds(s + 2, 1), t * P:(t + 1) * P, :].rearrange("a p n -> p (a n)")).then_inc(ADJ[t % 2], 16)
                def load_xh():
                    sp.dma_start(xh[:, :, :], graph(x, s + 2)).then_inc(s_x_in, 16)
                if first and main:
                    load_xh()
                if first:
                    load_adj(0)
                    load_adj(1)
                if first and not main:
                    load_xh()
                if prepare:
                    load_weights()
                if zero_row:
                    sp.dma_start(h_table[N:N + 1, :], agg[0:1, 0, :]).then_inc(s_zero_out, 16)
                if main:
                    for a in range(2):
                        for j, ready, n in ((0, s_part_ready, a + 1), (1, s_mid_ready, a + 1), (2, s_low_ready, a + 1)):
                            sp.wait_ge(ready, n)
                            r = (2 * j + a) * C
                            sp.dma_start(parts_d[r:r + C, :], parts[:, j, a, :]).then_inc(PARTS_OUT[j], 16)
                    for g in range(2):
                        for j in range(3):
                            if g == 0:
                                sp.wait_ge(PARTS_OUT[j], 32)
                            for i in range(len(Q_PART)):
                                for a, dst, part in ((0, qs, Q_PART[i]), (1, ks, K_PART[i])):
                                    if part == j:
                                        r = (2 * j + a) * C + g * GROUP * D
                                        sp.dma_start(dst[i * D:(i + 1) * D, g * GROUP:(g + 1) * GROUP, :],
                                                     parts_d[r:r + GROUP * D, :].rearrange("(h d) n -> d h n", d=D)).then_inc(QK_IN[g], 16)
                    sp.wait_ge(s_nflag_ready, 1)
                    wide = sp.value_load(nflag_i[0:1, 0:1], min_val=0, max_val=1)
                    with sp.If(wide > 0):
                        sp.wait_ge(s_gshift_parts, 1)
                        for j in range(3):
                            sp.dma_start(qs[SPLIT + j:SPLIT + j + 1, :, :].rearrange("p h (t n) -> p (h t) n", t=T), shp[:, j, :]).then_inc(s_shift_in, 16)
                if post:
                    for n, (lo, hi) in enumerate(pieces):
                        sp.wait_ge(s_out_ready, n + 1)
                        sp.dma_start(out[bass.ds(s - 1, 1), lo * P:hi * P, :].rearrange("a (t p) c -> p (a t) c", p=P), y2[:, lo:hi, :]).then_inc(s_out_stored, 16)
                if first:
                    for t in range(2, T):
                        load_adj(t)
                    sp.wait_ge(s_h_ready, T)
                    sp.dma_start(graph(h_rows, s + 2), xh[:, :, :]).then_inc(s_h_rows_out, 16)
                    if pooling:
                        sp.wait_ge(s_pooled_ready, T)
                    sp.dma_start(rows_of(h_table), xh[:, :, :]).then_inc(s_h_table_out, 16)
                    sp.wait_ge(s_h_rows_out, 16)
                    sp.wait_ge(s_h_table_out, 16)
                if zero_row:
                    sp.wait_ge(s_zero_out, 16)
                if prepare:
                    sp.wait_ge(s_w_in, W_LOADS)
                if post:
                    sp.wait_ge(s_out_stored, 16 * len(pieces))

            @block.gpsimd
            def _(pool):
                def keep():
                    if post:
                        pool.wait_ge(s_out_ready, 1)
                    pool.wait_ge(s_h2_near, TH)
                    nc.gpsimd.tensor_copy(x1p[:, :, :], x1[:, :, :]).then_inc(s_kept, 1)

                if pooling:
                    pool.wait_ge(s_lists_in, 16)
                    if main:
                        pool.wait_ge(s_ag_in, 16)

                    def send(t):
                        pool.wait_ge(s_pooled_ready, t + 1)
                        pool.indirect_dma_start(out=pooled[:, :], out_offset=bass.IndirectOffsetOnAxis(ap=lsorted[:, t, DEST:DEST + 1], axis=0),
                                                in_=agg[:, t % 2, :], in_offset=None).then_inc(OUT[t % 2], 16)
                    for t in range(T):
                        n = pool.value_load(lsorted[0:1, t, COUNT:COUNT + 1], min_val=0, max_val=S)
                        if t >= 2:
                            pool.wait_ge(s_nb_used, t - 1)

                        def gather(lo, hi):
                            for k in range(lo, hi):
                                pool.indirect_dma_start(out=nb[:, t % 2, k, :], out_offset=None, in_=h_table[:, :],
                                                        in_offset=bass.IndirectOffsetOnAxis(ap=lsorted[:, t, k:k + 1], axis=0)).then_inc(POOL[t], 16)
                        gather(0, sizes[0])
                        for lo, hi in zip(sizes, sizes[1:]):
                            with pool.If(n > lo):
                                gather(lo, hi)
                        if t >= 1:
                            send(t - 1)
                        if main and t == T - 2:
                            keep()
                if first:
                    pool.wait_ge(s_ranks, 2)
                    for t in range(T):
                        pool.indirect_dma_start(out=lists[:, :], out_offset=bass.IndirectOffsetOnAxis(ap=rank_i[:, t:t + 1], axis=0),
                                                in_=lst[:, t, :], in_offset=None).then_inc(s_lists_out, 16)
                if pooling:
                    send(T - 1)
                    pool.wait_ge(s_pooled_out0, 16 * TH)
                    pool.wait_ge(s_pooled_out1, 16 * TH)
                elif main:
                    keep()
                if first:
                    pool.wait_ge(s_lists_out, 16 * T)

            @block.vector
            def _(dve):
                ch = Chain(dve, s_dve_chain)

                def add_halves(dst, src, j, ready, used, tiles=(0, T)):
                    for h in range(tiles[0] // TH, tiles[1] // TH):
                        dve.wait_ge(ready, h + 1)
                        ch.step(nc.vector.tensor_tensor(dst[:, h * TH:(h + 1) * TH, :], src[:, h, :].rearrange("p (t c) -> p t c", t=TH),
                                                        rows[:, j:j + 1, :].to_broadcast([P, TH, C]), ALU.add))
                    ch.settle()
                    dve.sem_inc(used, 1)

                def row(j, tiles):
                    return rows[:, j:j + 1, :].to_broadcast([P, tiles[1] - tiles[0], C])

                def scaled(v, g, tiles):
                    for t in range(*tiles):
                        ch.step(nc.vector.tensor_scalar(v[:, t, :], v[:, t, :], nw3[:, 4, t:t + 1], nw3[:, 3, t:t + 1], ALU.mult, ALU.add))
                    ch.settle()
                    k = slice(*tiles)
                    ch.link(nc.vector.tensor_tensor(v[:, k, :], v[:, k, :], row(g, tiles), ALU.mult))

                def residual(n):
                    tiles = pieces[n]

                    def fill(h):
                        dve.wait_ge(s_proj_ready, h + 1)
                        ch.step(nc.vector.scalar_tensor_tensor(out=y[:, h * TH:(h + 1) * TH, :], in0=h2[:, h * TH:(h + 1) * TH, :], scalar=0.0,
                                                               in1=cb[:, h, :].rearrange("p (t c) -> p t c", t=TH), op0=ALU.max, op1=ALU.add))
                    if main:
                        moments(ch, y, st3, mv3, tiles, fill)
                        dve.sem_inc(s_y_filled, 1)
                    else:
                        row_stats(ch, y, st3, mv3, nw3, s_rstd3, tiles, fill)
                        dve.wait_ge(s_rstd3, n + 1)

                def z_rows(n):
                    tiles = pieces[n]
                    k = slice(*tiles)
                    scaled(y, G1, tiles)
                    nc.vector.tensor_tensor(y[:, k, :], y[:, k, :], row(B1R, tiles), ALU.add).then_inc(s_z_ready, 1)
                    dve.wait_ge(s_z_ready, n + 1)

                def finish(n):
                    tiles = pieces[n]
                    k = slice(*tiles)
                    add_halves(y2, ax, B2, s_ffn_ready, s_ffn_used, tiles)
                    ch.link(nc.vector.tensor_tensor(y2[:, k, :], y2[:, k, :], y[:, k, :], ALU.add))
                    row_stats(ch, y2, st3, mv3, nw3, s_rstd4, tiles)
                    dve.wait_ge(s_rstd4, n + 1)
                    scaled(y2, G2, tiles)
                    ch.link(nc.vector.tensor_tensor(y2[:, k, :], y2[:, k, :], row(B2R, tiles), ALU.add))
                    nc.vector.tensor_tensor(y2[:, k, :], y2[:, k, :], x1p[:, k, :], ALU.add).then_inc(s_out_ready, 1)

                def linear():
                    dve.wait_ge(s_x1_in, 16)

                    def fill(h):
                        dve.wait_ge(s_lin_ready, h + 1)
                        v = x1[:, h * TH:(h + 1) * TH, :]
                        ch.step(nc.vector.scalar_tensor_tensor(out=v, in0=sc[:, h, :].rearrange("p (t c) -> p t c", t=TH), scalar=0.0, in1=v,
                                                               op0=ALU.max, op1=ALU.add))
                    moments(ch, x1, st2, mv2, fill=fill)

                def next_h2():
                    dve.wait_ge(s_rstd2, 1)
                    for t in range(TH, T):
                        nc.vector.tensor_scalar(h2[:, t, :], x1[:, t, :], nw2[:, 4, t:t + 1], nw2[:, 3, t:t + 1], ALU.mult, ALU.add).then_inc(s_h2_far, 1)

                def qk_parts():
                    for a in range(2):
                        dve.wait_ge(s_qk_f, 2 * a + 2)
                        nc.vector.tensor_copy(parts[:, 0, a, :], qkf[:, a, :]).then_inc(s_part_ready, 1)
                        dve.wait_ge(s_part_ready, a + 1)
                        ch.link(nc.vector.tensor_tensor(resid[:, a, :], qkf[:, a, :], parts[:, 0, a, :], ALU.subtract))
                        nc.vector.tensor_copy(parts[:, 1, a, :], resid[:, a, :]).then_inc(s_mid_ready, 1)
                        dve.wait_ge(s_mid_ready, a + 1)
                        nc.vector.tensor_tensor(parts[:, 2, a, :], resid[:, a, :], parts[:, 1, a, :], ALU.subtract).then_inc(s_low_ready, 1)
                    bv = rows[:, BV:BV + 1, :].rearrange("p a (h d) -> p a h d", d=D).to_broadcast([P, TH, HEADS, D])
                    for h in range(2):
                        dve.wait_ge(s_v_ready, h + 1)
                        nc.vector.tensor_tensor(va[:, h * TH:(h + 1) * TH, :, 0:D], sc[:, 2 + h, :].rearrange("p (t h d) -> p t h d", t=TH, d=D),
                                                bv, ALU.add).then_inc(s_v_sb, 1)

                def norm_flag():
                    dve.wait_ge(s_norms_ready, 1)
                    ch.link(nc.vector.tensor_reduce(nrm[:, 0:2], sc[0:HEADS, :, :].rearrange("p (a b) n -> p a (b n)", a=2), AX.X, ALU.max))
                    nc.vector.tensor_tensor(nrm[:, 2:3], nrm[:, 0:1], nrm[:, 1:2], ALU.mult).then_inc(s_norms_max, 1)
                    dve.wait_ge(s_norm_row, 1)
                    ch.link(nc.vector.tensor_reduce(nflag[0:1, 0:1], sc[0:1, 0, 0:HEADS], AX.X, ALU.max))
                    nc.vector.tensor_scalar(nflag_i[0:1, 0:1], nflag[0:1, 0:1], SAFE, None, ALU.is_gt).then_inc(s_nflag_ready, 1)
                    dve.wait_ge(s_nflag_ready, 1)
                    return dve.value_load(nflag_i[0:1, 0:1], min_val=0, max_val=1)

                def wide_maxima(wide):
                    with dve.If(wide > 0):
                        for i in range(HEADS * T):
                            dve.wait_ge(s_gscores, i + 1)
                            nc.vector.tensor_reduce(shift[:, i:i + 1], sc[:, 2 * (i % 2):2 * (i % 2) + 2, :].rearrange("p a n -> p (a n)"),
                                                    AX.X, ALU.max).then_inc(s_gmax, 1)
                        dve.wait_ge(s_gmax, HEADS * T)
                        nc.vector.tensor_scalar(shift[:, :], shift[:, :], -1.0, None, ALU.mult).then_inc(s_gshift, 1)
                        dve.wait_ge(s_gshift_row, 1)
                        nc.vector.tensor_copy(shf[:, :], sc[0:HEADS * T, 0, 0:P]).then_inc(s_gshift, 1)
                        dve.wait_ge(s_gshift, 2)
                        nc.vector.tensor_copy(shp[:, 0, :], shf[:, :]).then_inc(s_gshift, 1)
                        dve.wait_ge(s_gshift, 3)
                        nc.vector.tensor_tensor(shr[:, :], shf[:, :], shp[:, 0, :], ALU.subtract).then_inc(s_gshift, 1)
                        dve.wait_ge(s_gshift, 4)
                        nc.vector.tensor_copy(shp[:, 1, :], shr[:, :]).then_inc(s_gshift, 1)
                        dve.wait_ge(s_gshift, 5)
                        nc.vector.tensor_tensor(shp[:, 2, :], shr[:, :], shp[:, 1, :], ALU.subtract).then_inc(s_gshift_parts, 1)

                def list_pair(t0):
                    pair = (t0, t0 + 1)
                    for t in pair:
                        dve.wait_ge(ADJ[t % 2], 16 * (t // 2 + 1))
                        if t == T - 1 and post:
                            dve.wait_ge(s_out_stored, 16)
                        nc.vector.scalar_tensor_tensor(out=keys[:, (t + 1) % T, :], in0=adj_t[:, t % 2, :], scalar=0.0, in1=prio,
                                                       op0=ALU.not_equal, op1=ALU.mult).then_inc(s_adj_used, 1)
                    done = {}
                    for t in pair:
                        dve.wait_ge(s_adj_used, t + 1)
                        for c in range(CHUNKS):
                            ch.step(nc.vector.max(cand[:, t, 8 * c:8 * c + 8], keys[:, (t + 1) % T, c * CW:(c + 1) * CW]))
                        done[t] = ch.n
                    for r in range(4):
                        for t in pair:
                            dve.wait_ge(s_dve_chain, done[t])
                            src = left[:, t % 2, :] if r else cand[:, t, :]
                            ch.step(nc.vector.max(vals[:, t, 8 * r:8 * r + 8], src))
                            done[t] = ch.n
                        if r < 3:
                            for t in pair:
                                dve.wait_ge(s_dve_chain, done[t])
                                src = left[:, t % 2, :] if r else cand[:, t, :]
                                ch.step(nc.vector.match_replace(out=left[:, t % 2, :], in_to_replace=vals[:, t, 8 * r:8 * r + 8], in_values=src, imm_value=0.0))
                                done[t] = ch.n
                    ch.settle()

                def pool_tile(t):
                    if t == 0:
                        dve.wait_ge(s_lists_in, 16)
                    n = dve.value_load(lsorted[0:1, t, COUNT:COUNT + 1], min_val=0, max_val=S)
                    if t >= 2:
                        dve.wait_ge(OUT[t % 2], 16 * (t // 2))
                    for j, m in enumerate(sizes):
                        low = sizes[j - 1] if j else -1
                        with dve.If(n > low):
                            with dve.If(n < (m + 1)):
                                dve.wait_ge(POOL[t], 16 * m)
                                nc.vector.tensor_reduce(agg[:, t % 2, :], nb[:, t % 2, 0:m, :].rearrange("p k c -> p c k"), AX.X, ALU.max).then_inc(s_pooled_ready, 1)
                    dve.wait_ge(s_pooled_ready, t + 1)
                    dve.sem_inc(s_nb_used, 1)

                def find_crowded():
                    eighth = cand[:, :, :].rearrange("p t (c k) -> p t c k", k=8)[:, :, :, 7]
                    ch.link(nc.vector.tensor_reduce(full[:, 1:1 + T], eighth, AX.X, ALU.max))
                    nc.vector.tensor_reduce(full[:, 0:1], full[:, 1:1 + T], AX.X, ALU.max).then_inc(s_full_ready, 1)

                def crowded_tiles():
                    dve.wait_ge(s_full_rows, 1)
                    ch.link(nc.vector.tensor_reduce(crowded[:, :], ax0[0:1 + T, 0:P], AX.X, ALU.max))
                    ch.link(nc.vector.tensor_copy(crowded_i[:, :], crowded[:, :]))
                    any_tile = dve.value_load(crowded_i[0:1, 0:1], min_val=0, max_val=N)
                    with dve.If(any_tile > 0):
                        for t in range(T):
                            again = dve.value_load(crowded_i[1 + t:2 + t, 0:1], min_val=0, max_val=N)
                            key = keys[:, (t + 1) % T, :]
                            with dve.If(again > 0):
                                for r in range(4):
                                    v = vals[:, t, 8 * r:8 * r + 8]
                                    nc.vector.max(v, key).then_inc(s_crowded, 1)
                                    dve.wait_ge(s_crowded, 8 * t + 2 * r + 1)
                                    nc.vector.match_replace(out=key, in_to_replace=v, in_values=key, imm_value=0.0).then_inc(s_crowded, 1)
                                    dve.wait_ge(s_crowded, 8 * t + 2 * r + 2)
                            with dve.If(again < 1):
                                dve.sem_inc(s_crowded, 8)

                def make_lists():
                    ch.link(nc.vector.tensor_scalar(rprod[:, :, 0:S], vals[:, :, 0:S], 0.0, None, ALU.is_gt))
                    ch.link(nc.vector.tensor_reduce(cnt[:, :], rprod[:, :, 0:S], AX.X, ALU.add))
                    levels = level[:, :].rearrange("p (a v) -> p a v", a=1).to_broadcast([P, T, COUNT])
                    counts = cnt[:, :].rearrange("p (t a) -> p t a", a=1).to_broadcast([P, T, COUNT])
                    ch.step(nc.vector.tensor_tensor(above[:, :, :], counts, levels, ALU.is_gt))
                    ch.link(nc.vector.tensor_tensor(onehot[:, :, :], counts, levels, ALU.is_equal))
                    ch.link(nc.vector.tensor_reduce(rprod[:, 0, :], above[:, :, :].rearrange("p t v -> p v t"), AX.X, ALU.add))
                    nc.vector.tensor_copy(abovesum[:, :], rprod[:, 0, :]).then_inc(s_rank_in, 1)
                    ch.step(nc.vector.tensor_scalar(lst[:, :, 0:S], vals[:, :, 0:S], -1.0, float(N), ALU.mult, ALU.add))
                    ch.link(nc.vector.tensor_copy(lst[:, :, DEST:DEST + 1], node_i[:, :].rearrange("p (t a) -> p t a", a=1)))
                    nc.vector.tensor_copy(lst[:, :, COUNT:COUNT + 1], cnt[:, :].rearrange("p (t a) -> p t a", a=1)).then_inc(s_ranks, 1)

                def list_ranks():
                    dve.wait_ge(s_rank_counts, 1)
                    dve.wait_ge(s_rank_in, 1)
                    dve.wait_ge(s_ranks, 1)
                    ch.link(nc.vector.tensor_tensor(rprod[:, :, :], ax1[:, 0:T * COUNT].rearrange("p (t v) -> p t v", t=T), onehot[:, :, :], ALU.mult))
                    ch.link(nc.vector.tensor_reduce(cnt[:, :], rprod[:, :, :], AX.X, ALU.add))
                    nc.vector.tensor_copy(rank_i[:, :], cnt[:, :]).then_inc(s_ranks, 1)

                def context(u):
                    qh, g = divmod(u, 2)
                    dve.wait_ge(s_ctxT_raw, u + 1)
                    c = ax0.rearrange("p (t g d) -> p t g d", t=TH, g=GROUP)
                    ch.link(nc.vector.reciprocal(rden[:, :, :], c[:, :, :, D]))
                    r = rden[:, :, :].rearrange("p t (g a) -> p t g a", a=1).to_broadcast([P, TH, GROUP, D])
                    o = ctxn[:, qh * TH:(qh + 1) * TH, g * GROUP * D:(g + 1) * GROUP * D].rearrange("p t (g d) -> p t g d", d=D)
                    nc.vector.tensor_tensor(o, c[:, :, :, 0:D], r, ALU.mult).then_inc(s_ctxn_ready, 1)

                if prepare:
                    nc.vector.memset(qs[96:128, :, :].rearrange("p h n -> p (h n)").bitcast(i32), 0)
                    nc.vector.memset(ks[96:128, :, :], 1.0)
                    nc.vector.memset(va[:, :, :, :], 1.0)
                    for g in range(3):
                        dve.wait_ge(s_wT_ready, g + 1)
                        if g == 0:
                            nc.vector.tensor_copy(wqkvT[:, :], sc[:, 0, 0:3 * C])
                            nc.vector.tensor_copy(woT[:, :], sc[:, 0, 3 * C:4 * C])
                        elif g == 1:
                            nc.vector.tensor_copy(w1T[:, :], sc[:, 1, :])
                        else:
                            nc.vector.tensor_copy(w2T[:, :, :], sc[:, 2, :].rearrange("p (c o) -> p c o", c=FC))
                def bar_rows(kt):
                    dve.wait_ge(s_bar_counts, kt + 1)
                    nc.vector.scalar_tensor_tensor(out=barred[:, kt, 0:HALF], in0=ax1, scalar=0.5, in1=m1[:, kt, 0:HALF],
                                                   op0=ALU.add, op1=ALU.is_gt).then_inc(s_bar_ready, 1)

                if post and main:
                    residual(0)
                if main:
                    linear()
                    inverse_roots(ch, mv23, nw23, slice(0, 2 * T if post else T), s_rstd2)
                    next_h2()
                if post and main:
                    z_rows(0)
                if main:
                    qk_parts()
                if pooling and main:
                    pool_tile(0)
                if prepare:
                    dve.wait_ge(s_x_in, 16)
                    row_stats(ch, xh, st1, mv1, nw1, s_rstd1)
                if main:
                    wide = norm_flag()
                    wide_maxima(wide)
                if pooling and main:
                    pool_tile(1)
                if post and not main:
                    for n in range(2):
                        residual(n)
                        z_rows(n)
                if post:
                    for n in range(len(pieces)):
                        finish(n)
                if first and main:
                    dve.wait_ge(s_x_in, 16)
                    row_stats(ch, xh, st1, mv1, nw1, s_rstd1)
                if pooling and main:
                    pool_tile(2)
                for t in range(0, T, 2):
                    if first:
                        list_pair(t)
                    if pooling:
                        pool_tile(t // 2 + (3 if main else 0))
                    if main and t in CONTEXT_AFTER:
                        context(CONTEXT_AFTER[t])
                if first:
                    find_crowded()
                    crowded_tiles()
                    make_lists()
                    list_ranks()
                if first and not pooling:
                    dve.wait_ge(s_x_in, 16)
                    row_stats(ch, xh, st1, mv1, nw1, s_rstd1)
                if pooling:
                    for t in range(T if main else TH, T):
                        pool_tile(t)
                if main:
                    context(2)
                if main and pooling:
                    pool_tile(T - 1)
                    for kt in range(T):
                        bar_rows(kt)
                if main:
                    context(3)
                    with dve.If(wide > 0):
                        nc.vector.memset(qs[96:128, :, :].rearrange("p h n -> p (h n)").bitcast(i32), 0)

            @block.scalar
            def _(act):
                def norm(dst, src, func, w, t, done):
                    nc.scalar.activation(dst[:, t, :], src[:, t, :], func, bias=w[:, 3, t:t + 1], scale=w[:, 4, t:t + 1]).then_inc(done, 1)

                def half_out(dst, src, h, ready, done, func=ACT.Copy):
                    act.wait_ge(ready, h + 1)
                    nc.scalar.activation(dst[:, h * HALF:(h + 1) * HALF], src[:, h, :], func).then_inc(done, 1)

                def halves_out(dst, src, ready, done, func=ACT.Copy):
                    for h in range(2):
                        half_out(dst, src, h, ready, done, func)

                def late_tile(kt):
                    act.wait_ge(s_late_counts, kt + 1)
                    nc.scalar.activation(barred[:, kt, HALF:N], cb[:, kt % 2, :], ACT.Relu, bias=1.0, scale=-1.0).then_inc(s_late_ready, 1)

                def load_mask(t):
                    if t:
                        act.wait_ge(s_m1_ready, t)
                    act.dma_start(adj_m[:, :], adj[bass.ds(s + 1, 1), t * P:(t + 1) * P, :].rearrange("a p n -> p (a n)")).then_inc(s_adj_mask_in, 16)

                def mask_tile(t):
                    act.wait_ge(s_adj_mask_in, 16 * (t + 1))
                    if t == 0 and main:
                        act.wait_ge(s_late_counts, T)
                    nc.scalar.activation(m1[:, t, :], adj_m[:, :], ACT.Relu).then_inc(s_m1_ready, 1)

                def bar_tile(kt):
                    act.wait_ge(s_bar_counts, kt + 1)
                    nc.scalar.activation(barred[:, kt, 0:HALF], ax1, ACT.Relu, bias=1.0, scale=-1.0).then_inc(s_bar_ready, 1)

                def first_norm(t):
                    if t == 0:
                        act.wait_ge(s_rstd1, 1)
                    norm(xh, xh, ACT.Relu, nw1, t, s_h_ready)

                if pooling:
                    load_mask(0)
                if post:
                    act.wait_ge(s_ctxT_ready, 1)
                    nc.scalar.activation(turned[:, HALF:N], sc[:, 1, :], ACT.Copy).then_inc(s_ctxT_sb, 1)
                if main:
                    halves_out(hT, sc[:, 2:4, :], s_hT_ready, s_hT_sb)
                    halves_out(aT, ax, s_aT_ready, s_aT_sb)
                    for kt in range(T):
                        late_tile(kt)
                    act.wait_ge(s_rstd2, 1)
                    for t in range(TH):
                        norm(h2, x1, ACT.Identity, nw2, t, s_h2_near)
                    halves_out(h2T, sc[:, 2:4, :], s_h2T_ready, s_h2T_sb, ACT.Relu)
                    for a, ready, bank in ((0, s_q_ready, ax), (1, s_k_ready, sc)):
                        for h in range(2):
                            act.wait_ge(ready, h + 1)
                            cols = slice(h * HALF, (h + 1) * HALF)
                            nc.scalar.activation(qkf[:, a, cols], bank[:, h, :], ACT.Identity, bias=bqk[:, a:a + 1]).then_inc(s_qk_f, 1)

                def hidden(i):
                    h, c = divmod(i, FC)
                    act.wait_ge(s_hid_ready, i + 1)
                    if h == 1:
                        act.wait_ge(s_ffn_ready, 1)
                    nc.scalar.activation(hid[:, c, :], hid_bank(i), ACT.Relu, bias=b1c[:, c:c + 1]).then_inc(s_hid_sb, 1)

                if post and main:
                    halves_out(turned, zbank, s_zT_ready, s_zT_sb)
                def hidden_half(h):
                    if not main:
                        half_out(turned, zbank, h, s_zT_ready, s_zT_sb)
                    for i in range(h * FC, (h + 1) * FC):
                        hidden(i)

                if post:
                    hidden_half(0)
                if main:
                    act.wait_ge(s_qk_f, 4)
                    act.wait_ge(s_v_ready, 2)
                    nc.scalar.activation(sq, qkf, ACT.Square).then_inc(s_sq_ready, 1)
                if post:
                    hidden_half(1)
                if main:
                    for u in range(UNITS):
                        for j in range(PAIRS):
                            i = u * PAIRS + j
                            act.wait_ge(s_scores_ready, i + 1)
                            if i >= 4:
                                act.wait_ge(s_pv_done, (i - 4) // 2 + 1)
                            nc.scalar.activation(probs[:, i % 4, :, :], sc[:, 2 * (i % 2):2 * (i % 2) + 2, :], ACT.Exp, scale=SCALE).then_inc(s_probs_ready, 1)
                            if i == TURN_AT + 1:
                                if first:
                                    act.wait_ge(s_rank_in, 1)
                                if post:
                                    act.wait_ge(s_out_stored, 16)
                                act.wait_ge(s_near_turned, 1)
                                nc.scalar.activation(turned[:, 0:HALF], ax0, ACT.Copy).then_inc(s_near_sb, 1)
                            if u >= 1 and j == 3:
                                if u >= 2:
                                    act.wait_ge(s_ctxT_raw, u - 1)
                                act.wait_ge(s_pv_done, u * T)
                                nc.scalar.activation(ctx_raw[:, :], cb[:, (u - 1) % 2, :], ACT.Copy).then_inc(s_ctx_sb, 1)
                            if first and i < NORM_FROM + MASK_EVERY * T and i % MASK_EVERY == 3 and i >= NORM_FROM:
                                first_norm((i - NORM_FROM) // MASK_EVERY)
                            if pooling and i // MASK_EVERY < T and i % MASK_EVERY == 1:
                                mask_tile(i // MASK_EVERY)
                            if pooling and i // MASK_EVERY < T - 1 and i % MASK_EVERY == 2:
                                load_mask(i // MASK_EVERY + 1)
                    act.wait_ge(s_ctxT_raw, 3)
                    act.wait_ge(s_pv_done, UNITS * T)
                    nc.scalar.activation(ctx_raw[:, :], cb[:, 1, :], ACT.Copy).then_inc(s_ctx_sb, 1)
                else:
                    if first:
                        for t in range(T):
                            first_norm(t)
                    if pooling:
                        for t in range(T):
                            if t:
                                load_mask(t)
                            mask_tile(t)
                        for kt in range(T):
                            bar_tile(kt)

            @block.tensor
            def _(pe):
                def keep_warm(bank, n):
                    for _ in range(n):
                        nc.tensor.matmul(bank, onesb[:, :], barred[:, 0, 0:HALF], start=True, stop=True)

                def bias_rows(banks, j):
                    for h in range(2):
                        nc.tensor.matmul(banks[:, h, :], ones_row[:, :], rows[0:1, j:j + 1, :].to_broadcast([1, TH, C]), start=True, stop=False)

                def transposes(dst, src, h, done):
                    for t in range(TH):
                        last = nc.tensor.transpose(dst[:, t * C:(t + 1) * C], src[:, h * TH + t, :], identf[:, :])
                    last.then_inc(done, 1)

                def count_edges(o, half, kt, done):
                    nc.tensor.matmul(o, identb[:, :], m1[:, kt, half * HALF:(half + 1) * HALF], start=True, stop=False)
                    if kt // TH == half:
                        a = kt % TH * P
                        nc.tensor.matmul(o[:, a:a + P], identb[:, :], identb[:, :], start=False, stop=False)
                    for j in range(TH):
                        last = nc.tensor.matmul(o[:, j * P:(j + 1) * P], m1[:, half * TH + j, kt * P:(kt + 1) * P], identb[:, :],
                                                start=False, stop=(j == TH - 1))
                    last.then_inc(done, 1)

                def bar_counts(kt):
                    pe.wait_ge(s_m1_ready, max(kt + 1, TH))
                    if kt:
                        pe.wait_ge(s_bar_ready, kt)
                    elif main and post:
                        pe.wait_ge(s_ffn_used, 1)
                    count_edges(ax1, 0, kt, s_bar_counts)

                def bar_edges(kt):
                    if kt == 0:
                        pe.wait_ge(s_m1_ready, T)
                        if post:
                            pe.wait_ge(s_ffn_used, 1)
                        if first:
                            pe.wait_ge(s_ranks, 2)
                    else:
                        pe.wait_ge(s_bar_ready, kt)
                    for j in range(TH):
                        last = nc.tensor.matmul(ax1[:, j * P:(j + 1) * P], m1[:, j, kt * P:(kt + 1) * P], negident[:, :],
                                                start=(j == 0), stop=(j == TH - 1 and kt >= TH))
                    if kt < TH:
                        last = nc.tensor.matmul(ax1[:, kt * P:(kt + 1) * P], identb[:, :], negident[:, :], start=False, stop=True)
                    last.then_inc(s_bar_counts, 1)

                def late_counts(kt):
                    if kt >= 2:
                        pe.wait_ge(s_late_ready, kt - 1)
                    elif post:
                        pe.wait_ge(s_y_filled, 1)
                    count_edges(cb[:, kt % 2, :], 1, kt, s_late_counts)

                def full_rows():
                    pe.wait_ge(s_full_ready, 1)
                    if main:
                        pe.wait_ge(s_ctxn_ready, 2)
                    nc.tensor.transpose(ax0[0:1 + T, 0:P], full[:, :], identf[:, :]).then_inc(s_full_rows, 1)

                def rank_counts():
                    pe.wait_ge(s_rank_in, 1)
                    if not main and pooling:
                        pe.wait_ge(s_bar_ready, T)
                    for t in range(T):
                        o = ax1[:, t * COUNT:(t + 1) * COUNT]
                        nc.tensor.matmul(o, onesb[:, :], abovesum[:, :], start=True, stop=False)
                        for e in range(t):
                            nc.tensor.matmul(o, onesb[:, :], onehot[:, e, :], start=False, stop=False)
                        last = nc.tensor.matmul(o, before[:, :], onehot[:, t, :], start=False, stop=True)
                    last.then_inc(s_rank_counts, 1)

                def scores(i):
                    u, j = divmod(i, PAIRS)
                    qh, g = divmod(u, 2)
                    kt, pair = divmod(j, 2)
                    if i >= 2:
                        pe.wait_ge(s_probs_ready, i - 1)
                    if i == PAIRS:
                        pe.wait_ge(s_qk_in1, QK_LOADS)
                    q = slice(qh * HALF, (qh + 1) * HALF)
                    for a in range(2):
                        h = g * GROUP + pair * 2 + a
                        o = sc[:, 2 * (i % 2) + a, :]
                        nc.tensor.matmul(o, ks[0:SPLIT + SHIFT, h, kt * P:(kt + 1) * P], qs[0:SPLIT + SHIFT, h, q], start=True, stop=False)
                    for a in range(2):
                        o = sc[:, 2 * (i % 2) + a, :]
                        last = nc.tensor.matmul(o, negident[:, :], barred[:, kt, q], start=False, stop=True)
                    last.then_inc(s_scores_ready, 1)

                def contexts(i):
                    u, kt = divmod(i, T)
                    g = u % 2
                    if kt == 0 and u >= 2:
                        pe.wait_ge(s_ctx_sb, u - 1)
                    pe.wait_ge(s_probs_ready, 2 * i + 2)
                    for a in range(GROUP):
                        last = nc.tensor.matmul(cb[SPAN * a:SPAN * (a + 1), u % 2, :], va[:, kt, g * GROUP + a, :],
                                                probs[:, (2 * i + a // 2) % 4, a % 2, :], start=(kt == 0), stop=(kt == T - 1))
                    last.then_inc(s_pv_done, 1)

                def context_rows(u):
                    pe.wait_ge(s_ctx_sb, u + 1)
                    if u:
                        pe.wait_ge(s_ctxn_ready, u)
                    elif post:
                        pe.wait_ge(s_ffn_used, 1)
                    if u == 3:
                        pe.wait_ge(s_near_sb, 1)
                    if u == 2 and first:
                        pe.wait_ge(s_rank_in, 1)
                    for t in range(TH):
                        last = nc.tensor.transpose(ax0[:, t * P:(t + 1) * P], ctx_raw[:, t * P:(t + 1) * P], identf[:, :])
                    last.then_inc(s_ctxT_raw, 1)

                def turn_z():
                    pe.wait_ge(s_late_ready, T)
                    pe.wait_ge(s_z_ready, 1)
                    for h in range(2):
                        transposes(zbank[:, h, :], y, h, s_zT_ready)

                def hidden(i):
                    h, c = divmod(i, FC)
                    if i in (0, FC):
                        pe.wait_ge(s_zT_sb, 2 if main else h + 1)
                    if main and i in (2, 3):
                        pe.wait_ge(s_qk_f, 4)
                    elif i >= 2:
                        pe.wait_ge(s_hid_sb, i - 1)
                    nc.tensor.matmul(hid_bank(i), w1T[:, c * P:(c + 1) * P], turned[:, h * HALF:(h + 1) * HALF], start=True, stop=True).then_inc(s_hid_ready, 1)

                def forward(h):
                    pe.wait_ge(s_hid_sb, (h + 1) * FC)
                    if main:
                        pe.wait_ge(s_qk_f, 2)
                    for t in range(TH):
                        for c in range(FC):
                            last = nc.tensor.matmul(ax[:, h, t * C:(t + 1) * C], hid[:, c, t * P:(t + 1) * P], w2T[:, c, :], start=(c == 0), stop=(c == FC - 1))
                    last.then_inc(s_ffn_ready, 1)

                if prepare:
                    pe.wait_ge(s_w_in, W_LOADS)
                    for g in range(3):
                        for j in range(4):
                            k = 4 * g + j
                            last = nc.tensor.transpose(sc[:, g, j * C:(j + 1) * C], wstage[:, k * C:(k + 1) * C], identf[:, :])
                        last.then_inc(s_wT_ready, 1)
                def project():
                    bias_rows(cb, BO)
                    for h in range(2):
                        if h == 1:
                            pe.wait_ge(s_ctxT_sb, 1)
                        for t in range(TH):
                            cols = slice((h * TH + t) * P, (h * TH + t + 1) * P)
                            last = nc.tensor.matmul(cb[:, h, t * C:(t + 1) * C], turned[:, cols], woT[:, :], start=False, stop=(t == TH - 1))
                        last.then_inc(s_proj_ready, 1)

                if post:
                    transposes(sc[:, 1, :], ctxn, 1, s_ctxT_ready)
                    project()
                if main:
                    pe.wait_ge(s_hl_in, 16)
                    for h in range(2):
                        transposes(sc[:, 2 + h, :], hl, h, s_hT_ready)
                    pe.wait_ge(s_ag_in, 16)
                    for h in range(2):
                        transposes(ax[:, h, :], ag, h, s_aT_ready)
                    bias_rows(sc, L0B)
                    pe.wait_ge(s_hT_sb, 2)
                    pe.wait_ge(s_aT_sb, 2)
                    for h in range(2):
                        for t in range(TH):
                            cols = slice((h * TH + t) * P, (h * TH + t + 1) * P)
                            o = sc[:, h, t * C:(t + 1) * C]
                            nc.tensor.matmul(o, hT[:, cols], w_l0[:, 0, :], start=False, stop=False)
                            last = nc.tensor.matmul(o, aT[:, cols], w_l0[:, 1, :], start=False, stop=(t == TH - 1))
                        last.then_inc(s_lin_ready, 1)
                    for kt in range(T):
                        late_counts(kt)
                    keep_warm(ax0, WARM_STATS)
                    for h in range(2):
                        pe.wait_ge((s_h2_near, s_h2_far)[h], TH)
                        transposes(sc[:, 2 + h, :], h2, h, s_h2T_ready)
                    for h in range(2):
                        pe.wait_ge(s_h2T_sb, h + 1)
                        nc.tensor.matmul(ax[:, h, :], wqkvT[:, 0:C], h2T[:, h * HALF:(h + 1) * HALF], start=True, stop=True).then_inc(s_q_ready, 1)
                    for h in range(2):
                        nc.tensor.matmul(sc[:, h, :], wqkvT[:, C:2 * C], h2T[:, h * HALF:(h + 1) * HALF], start=True, stop=True).then_inc(s_k_ready, 1)
                    if post:
                        turn_z()
                    for h in range(2):
                        for t in range(TH):
                            cols = slice((h * TH + t) * P, (h * TH + t + 1) * P)
                            last = nc.tensor.matmul(sc[:, 2 + h, t * C:(t + 1) * C], h2T[:, cols], wqkvT[:, 2 * C:3 * C], start=True, stop=True)
                        last.then_inc(s_v_ready, 1)
                if post:
                    if not main:
                        pe.wait_ge(s_z_ready, 1)
                        transposes(zbank[:, 0, :], y, 0, s_zT_ready)
                    for i in range(FC):
                        hidden(i)
                    forward(0)
                if main:
                    pe.wait_ge(s_sq_ready, 1)
                    pe.wait_ge(s_v_sb, 2)
                    for a in range(2):
                        for h in range(2):
                            last = nc.tensor.matmul(sc[0:HEADS, 2 * a + h, :], head_sum[:, :], sq[:, a, h * HALF:(h + 1) * HALF], start=True, stop=True)
                    last.then_inc(s_norms_ready, 1)
                if post and not main:
                    pe.wait_ge(s_z_ready, 2)
                    transposes(zbank[:, 1, :], y, 1, s_zT_ready)
                if post:
                    for i in range(FC, 2 * FC):
                        hidden(i)
                if main:
                    pe.wait_ge(s_norms_max, 1)
                    nc.tensor.transpose(sc[0:1, 0, 0:HEADS], nrm[:, 2:3], identf[0:HEADS, 0:HEADS]).then_inc(s_norm_row, 1)
                if post:
                    forward(1)
                if main:
                    pe.wait_ge(s_qk_in0, QK_LOADS)
                    pe.wait_ge(s_late_ready, T)
                    pe.wait_ge(s_nflag_ready, 1)
                    wide = pe.value_load(nflag_i[0:1, 0:1], min_val=0, max_val=1)
                    with pe.If(wide > 0):
                        pe.wait_ge(s_qk_in1, QK_LOADS)
                        for i in range(HEADS * T):
                            h, qt = divmod(i, T)
                            if i >= 2:
                                pe.wait_ge(s_gmax, i - 1)
                            for a in range(2):
                                nc.tensor.matmul(sc[:, 2 * (i % 2) + a, :], qs[0:SPLIT, h, qt * P:(qt + 1) * P], ks[0:SPLIT, h, a * HALF:(a + 1) * HALF],
                                                 start=True, stop=False)
                                last = nc.tensor.matmul(sc[:, 2 * (i % 2) + a, :], negident[:, :], barred[:, qt, a * HALF:(a + 1) * HALF], start=False, stop=True)
                            last.then_inc(s_gscores, 1)
                        pe.wait_ge(s_gshift, 1)
                        nc.tensor.transpose(sc[0:HEADS * T, 0, 0:P], shift[:, :], identf[:, :]).then_inc(s_gshift_row, 1)
                        pe.wait_ge(s_shift_in, 48)

                    for i in range(UNITS * PAIRS):
                        u, j = divmod(i, PAIRS)
                        scores(i)
                        if i >= 3 and i % 2 == 1:
                            contexts((i - 3) // 2)
                        if u >= 1 and j == ROWS_AT[u]:
                            context_rows(u - 1)
                        if pooling and i >= BARS_FROM:
                            bar_edges(i - BARS_FROM)
                        if i == TURN_AT:
                            pe.wait_ge(s_ctxn_ready, 3)
                            transposes(ax0, ctxn, 0, s_near_turned)
                        if first and i == FULL_AT:
                            full_rows()
                        if first and i == RANKS_AT:
                            rank_counts()
                    if pooling:
                        for kt in range(UNITS * PAIRS - BARS_FROM, T):
                            bar_edges(kt)
                    contexts(UNITS * T - 1)
                    if pooling:
                        pe.wait_ge(s_bar_ready, T)
                    keep_warm(ax1, WARM_END)
                    context_rows(3)
                    keep_warm(ax1, WARM_END)
                else:
                    if pooling:
                        for kt in range(T):
                            bar_counts(kt)
                    if first:
                        full_rows()
                        rank_counts()
            block_ctx.__exit__(None, None, None)
            clear_semaphores()

        slot(-2, True, False, False, False)
        slot(-1, True, True, False, False)
        slot(0, True, True, True, False)
        with nc.Fori(0, B - 3) as i:
            slot(i + 1, True, True, True, True)
        slot(B - 2, False, True, True, True)
        slot(B - 1, False, False, True, True)
        slot(B, False, False, False, True)


_INS = ['x', 'adj', 'L0_gnn_W', 'L0_gnn_b', 'L1_gnn_Wqkv', 'L1_gnn_bqkv', 'L1_gnn_Wo', 'L1_gnn_bo', 'L1_gnn_ln1_g', 'L1_gnn_ln1_b',
        'L1_gnn_W1', 'L1_gnn_b1', 'L1_gnn_W2', 'L1_gnn_b2', 'L1_gnn_ln2_g', 'L1_gnn_ln2_b']
_OUTS = [((B, N, C), 'float32')]


def kernel(**inputs):
    import numpy as _np
    import concourse.bacc as _bacc
    from concourse import mybir as _mybir
    from concourse.bass_utils import run_bass_kernel_spmd as _run

    nc = _bacc.Bacc("TRN2", target_bir_lowering=False, num_devices=1)
    arrays, args = {}, []
    for name in _INS:
        a = _np.ascontiguousarray(inputs[name])
        arrays[f"in_{name}_dram"] = a
        args.append(nc.dram_tensor(f"in_{name}_dram", a.shape, _mybir.dt.from_np(a.dtype), kind="ExternalInput").ap())
    for i, (shape, dtype) in enumerate(_OUTS):
        dt = _mybir.dt.from_np(_np.dtype(dtype))
        args.append(nc.dram_tensor(f"out_{i}_dram", shape, dt, kind="ExternalOutput").ap())
    program(nc, *args)
    r = _run(nc, [arrays], core_ids=[0])
    return r.results[0]["out_0_dram"]
```
